# Optimizing a Trainium2 kernel written in Bass

```python
import numpy as np
import jax
import jax.numpy as jnp

def _softmax(x, axis=-1):
    return jax.nn.softmax(x, axis=axis)

def _gelu(x):
    return jax.nn.gelu(x, approximate=True)

def _silu(x):
    return jax.nn.silu(x)

def _sigmoid(x):
    return jax.nn.sigmoid(x)

def _layernorm(x, axis=-1, eps=1e-05):
    m = jnp.mean(x, axis=axis, keepdims=True)
    v = jnp.var(x, axis=axis, keepdims=True)
    return (x - m) / jnp.sqrt(v + eps)

def _scatter_add(tgt, idx, src, axis=0):
    return tgt.at[idx].add(src)

def _segment_sum(src, seg, n):
    return jax.ops.segment_sum(src, seg, n)
kernel_name = 'mk_vit_tower_d1_tok_img1024_r4_9dff96'

def setup_inputs(seed: int=0):
    np.random.seed(seed)
    _w = jnp.asarray

    def _rec_inputs():
        import jax
        import jax.numpy as jnp
        _rk = jax.random.key(seed)
        x = -0.00016672 + 0.999947 * jax.random.normal(jax.random.fold_in(_rk, 1), (64, 3, 96, 96), jnp.float32)
        return x
    x = _rec_inputs()

    def _L0_tok_setup():
        import jax, jax.numpy as jnp
        import numpy as np
        key = jax.random.key(seed)
        kx, kw, kpos = jax.random.split(key, 3)
        B, C, H, W = (64, 3, 96, 96)
        p, dim = (16, 256)
        n_patches = H // p * (W // p)
        x = jax.random.normal(kx, (B, C, H, W), dtype=jnp.float32)
        w = jax.random.normal(kw, (dim, C * p * p), dtype=jnp.float32) * 0.02
        b = jnp.zeros((dim,), dtype=jnp.float32)
        cls_token = jnp.ones((dim,), dtype=jnp.float32)
        pos = jax.random.uniform(kpos, (n_patches + 1, dim), dtype=jnp.float32)
        return {'x': x, 'w': w, 'b': b, 'cls_token': cls_token, 'pos': pos, 'patch_size': p}
    _L0_tok_all = _L0_tok_setup()
    _L0_tok_in = {k: v for k, v in _L0_tok_all.items() if k in ('w', 'b', 'cls_token', 'pos')}
    del _L0_tok_all

    def _L0_attn_setup():
        import jax, jax.numpy as jnp
        import numpy as np
        import math
        N_EMBD = 256
        N_LAYER = 24
        LAYER_ID = 12
        B, T = (8, 512)

        def _init_params():
            C = N_EMBD
            ratio_0_to_1 = LAYER_ID / (N_LAYER - 1)
            ratio_1_to_almost0 = 1.0 - LAYER_ID / N_LAYER
            h = np.arange(C, dtype=np.float64)
            decay_speed = -5.0 + 8.0 * (h / (C - 1)) ** (0.7 + 1.3 * ratio_0_to_1)
            zigzag = ((np.arange(C) + 1) % 3 - 1) * 0.5
            time_first = np.ones(C) * math.log(0.3) + zigzag
            xline = (np.arange(C, dtype=np.float64) / C).reshape(1, 1, C)
            time_mix_k = xline ** ratio_1_to_almost0
            time_mix_v = xline ** ratio_1_to_almost0 + 0.3 * ratio_0_to_1
            time_mix_r = xline ** (0.5 * ratio_1_to_almost0)
            f32 = lambda a: jnp.asarray(a, dtype=jnp.float32)
            return (f32(decay_speed), f32(time_first), f32(time_mix_k), f32(time_mix_v), f32(time_mix_r))

        def _wkv(w, u, k, v):
            kT = jnp.swapaxes(k, 0, 1)
            vT = jnp.swapaxes(v, 0, 1)

            def step(carry, kv_t):
                p, q, o = carry
                kt, vt = kv_t
                no = jnp.maximum(o, u + kt)
                A = jnp.exp(o - no)
                Bc = jnp.exp(u + kt - no)
                y = (A * p + Bc * vt) / (A * q + Bc)
                no2 = jnp.maximum(w + o, kt)
                A2 = jnp.exp(w + o - no2)
                B2 = jnp.exp(kt - no2)
                return ((A2 * p + B2 * vt, A2 * q + B2, no2), y)
            z = jnp.zeros(k.shape[::2], dtype=k.dtype)
            init = (z, z, jnp.full_like(z, -1e+38))
            _, yT = jax.lax.scan(step, init, (kT, vT))
            return jnp.swapaxes(yT, 0, 1)
        key = jax.random.key(seed)
        kx, kk, kv, kr, ko = jax.random.split(key, 5)
        C = N_EMBD
        scale = 1.0 / np.sqrt(C)
        time_decay, time_first, tmk, tmv, tmr = _init_params()
        return {'x': jax.random.normal(kx, (B, T, C), dtype=jnp.float32), 'time_decay': time_decay, 'time_first': time_first, 'time_mix_k': tmk, 'time_mix_v': tmv, 'time_mix_r': tmr, 'W_key': jax.random.uniform(kk, (C, C), jnp.float32, -scale, scale), 'W_value': jax.random.uniform(kv, (C, C), jnp.float32, -scale, scale), 'W_receptance': jax.random.uniform(kr, (C, C), jnp.float32, -scale, scale), 'W_output': jax.random.uniform(ko, (C, C), jnp.float32, -scale, scale)}
    _L0_attn_all = _L0_attn_setup()
    _L0_attn_in = {k: v for k, v in _L0_attn_all.items() if k in ('time_decay', 'time_first', 'time_mix_k', 'time_mix_v', 'time_mix_r', 'W_key', 'W_value', 'W_receptance', 'W_output')}
    del _L0_attn_all

    def _L0_ffn_setup():
        import jax, jax.numpy as jnp
        import numpy as np
        E = 8
        H = 256
        M = 512
        K = 2
        SE = 1
        BSZ, SEQ = (2, 256)
        W_SCALE = 0.02
        key = jax.random.key(seed)
        ks = jax.random.split(key, 9)
        return {'x': jax.random.normal(ks[0], (BSZ, SEQ, H), jnp.float32), 'gate_w': jax.random.normal(ks[1], (E, H), jnp.float32) * W_SCALE, 'beta': jnp.zeros((E,), jnp.float32), 'gate_proj_w': jax.random.normal(ks[2], (E, H, M), jnp.float32) * W_SCALE, 'up_proj_w': jax.random.normal(ks[3], (E, H, M), jnp.float32) * W_SCALE, 'down_proj_w': jax.random.normal(ks[4], (E, M, H), jnp.float32) * W_SCALE, 'shared_gate_w': jax.random.normal(ks[5], (SE, H, M), jnp.float32) * W_SCALE, 'shared_up_w': jax.random.normal(ks[6], (SE, H, M), jnp.float32) * W_SCALE, 'shared_down_w': jax.random.normal(ks[7], (SE, M, H), jnp.float32) * W_SCALE}
    _L0_ffn_all = _L0_ffn_setup()
    _L0_ffn_in = {k: v for k, v in _L0_ffn_all.items() if k in ('gate_w', 'beta', 'gate_proj_w', 'up_proj_w', 'down_proj_w', 'shared_gate_w', 'shared_up_w', 'shared_down_w')}
    del _L0_ffn_all
    return {'x': x, 'L0_tok_w': _L0_tok_in['w'], 'L0_tok_b': _L0_tok_in['b'], 'L0_tok_cls_token': _L0_tok_in['cls_token'], 'L0_tok_pos': _L0_tok_in['pos'], 'L0_attn_time_decay': _L0_attn_in['time_decay'], 'L0_attn_time_first': _L0_attn_in['time_first'], 'L0_attn_time_mix_k': _L0_attn_in['time_mix_k'], 'L0_attn_time_mix_v': _L0_attn_in['time_mix_v'], 'L0_attn_time_mix_r': _L0_attn_in['time_mix_r'], 'L0_attn_W_key': _L0_attn_in['W_key'], 'L0_attn_W_value': _L0_attn_in['W_value'], 'L0_attn_W_receptance': _L0_attn_in['W_receptance'], 'L0_attn_W_output': _L0_attn_in['W_output'], 'L0_ffn_gate_w': _L0_ffn_in['gate_w'], 'L0_ffn_beta': _L0_ffn_in['beta'], 'L0_ffn_gate_proj_w': _L0_ffn_in['gate_proj_w'], 'L0_ffn_up_proj_w': _L0_ffn_in['up_proj_w'], 'L0_ffn_down_proj_w': _L0_ffn_in['down_proj_w'], 'L0_ffn_shared_gate_w': _L0_ffn_in['shared_gate_w'], 'L0_ffn_shared_up_w': _L0_ffn_in['shared_up_w'], 'L0_ffn_shared_down_w': _L0_ffn_in['shared_down_w']}

def reference(x, L0_tok_w, L0_tok_b, L0_tok_cls_token, L0_tok_pos, L0_attn_time_decay, L0_attn_time_first, L0_attn_time_mix_k, L0_attn_time_mix_v, L0_attn_time_mix_r, L0_attn_W_key, L0_attn_W_value, L0_attn_W_receptance, L0_attn_W_output, L0_ffn_gate_w, L0_ffn_beta, L0_ffn_gate_proj_w, L0_ffn_up_proj_w, L0_ffn_down_proj_w, L0_ffn_shared_gate_w, L0_ffn_shared_up_w, L0_ffn_shared_down_w):
    import jax
    import jax.numpy as jnp

    def _L0_tok_ref(x, w, b, cls_token, pos, patch_size):
        import jax, jax.numpy as jnp
        import numpy as np
        B, C, H, W = x.shape
        p = patch_size
        Hp, Wp = (H // p, W // p)
        dim = w.shape[0]
        patches = x.reshape(B, C, Hp, p, Wp, p).transpose(0, 2, 4, 1, 3, 5).reshape(B, Hp * Wp, C * p * p)
        tokens = jnp.einsum('bnf,df->bnd', patches, w) + b
        cls = jnp.broadcast_to(cls_token, (B, 1, dim))
        emb = jnp.concatenate([cls, tokens], axis=1)
        return emb + pos

    def _L0_attn_ref(x, time_decay, time_first, time_mix_k, time_mix_v, time_mix_r, W_key, W_value, W_receptance, W_output):
        import jax, jax.numpy as jnp
        import numpy as np
        import math
        N_EMBD = 256
        N_LAYER = 24
        LAYER_ID = 12
        B, T = (8, 512)

        def _init_params():
            C = N_EMBD
            ratio_0_to_1 = LAYER_ID / (N_LAYER - 1)
            ratio_1_to_almost0 = 1.0 - LAYER_ID / N_LAYER
            h = np.arange(C, dtype=np.float64)
            decay_speed = -5.0 + 8.0 * (h / (C - 1)) ** (0.7 + 1.3 * ratio_0_to_1)
            zigzag = ((np.arange(C) + 1) % 3 - 1) * 0.5
            time_first = np.ones(C) * math.log(0.3) + zigzag
            xline = (np.arange(C, dtype=np.float64) / C).reshape(1, 1, C)
            time_mix_k = xline ** ratio_1_to_almost0
            time_mix_v = xline ** ratio_1_to_almost0 + 0.3 * ratio_0_to_1
            time_mix_r = xline ** (0.5 * ratio_1_to_almost0)
            f32 = lambda a: jnp.asarray(a, dtype=jnp.float32)
            return (f32(decay_speed), f32(time_first), f32(time_mix_k), f32(time_mix_v), f32(time_mix_r))

        def _wkv(w, u, k, v):
            kT = jnp.swapaxes(k, 0, 1)
            vT = jnp.swapaxes(v, 0, 1)

            def step(carry, kv_t):
                p, q, o = carry
                kt, vt = kv_t
                no = jnp.maximum(o, u + kt)
                A = jnp.exp(o - no)
                Bc = jnp.exp(u + kt - no)
                y = (A * p + Bc * vt) / (A * q + Bc)
                no2 = jnp.maximum(w + o, kt)
                A2 = jnp.exp(w + o - no2)
                B2 = jnp.exp(kt - no2)
                return ((A2 * p + B2 * vt, A2 * q + B2, no2), y)
            z = jnp.zeros(k.shape[::2], dtype=k.dtype)
            init = (z, z, jnp.full_like(z, -1e+38))
            _, yT = jax.lax.scan(step, init, (kT, vT))
            return jnp.swapaxes(yT, 0, 1)
        xx = jnp.concatenate([jnp.zeros_like(x[:, :1]), x[:, :-1]], axis=1)
        xk = x * time_mix_k + xx * (1.0 - time_mix_k)
        xv = x * time_mix_v + xx * (1.0 - time_mix_v)
        xr = x * time_mix_r + xx * (1.0 - time_mix_r)
        k = jnp.einsum('btc,dc->btd', xk, W_key)
        v = jnp.einsum('btc,dc->btd', xv, W_value)
        r = jnp.einsum('btc,dc->btd', xr, W_receptance)
        sr = jax.nn.sigmoid(r)
        w = -jnp.exp(time_decay)
        wkv = _wkv(w, time_first, k, v)
        return jnp.einsum('btc,dc->btd', sr * wkv, W_output)

    def _L0_ffn_ref(x, gate_w, beta, gate_proj_w, up_proj_w, down_proj_w, shared_gate_w, shared_up_w, shared_down_w):
        import jax, jax.numpy as jnp
        import numpy as np
        E = 8
        H = 256
        M = 512
        K = 2
        SE = 1
        BSZ, SEQ = (2, 256)
        W_SCALE = 0.02
        B0, S0, H0 = x.shape
        xt = x.reshape(-1, H0)
        B = xt.shape[0]
        logits = xt @ gate_w.T
        _, idx = jax.lax.top_k(logits + beta, K)
        probs = jax.nn.sigmoid(jnp.take_along_axis(logits, idx, axis=-1))
        c = jnp.zeros((B, E), xt.dtype).at[jnp.arange(B)[:, None], idx].add(probs)
        g = jnp.einsum('bh,ehm->bem', xt, gate_proj_w)
        u = jnp.einsum('bh,ehm->bem', xt, up_proj_w)
        h = jax.nn.silu(g) * u
        eo = jnp.einsum('bem,emh->beh', h, down_proj_w)
        combined = jnp.einsum('beh,be->bh', eo, c)
        sg = jnp.einsum('bh,ehm->bem', xt, shared_gate_w)
        su = jnp.einsum('bh,ehm->bem', xt, shared_up_w)
        sh = jax.nn.silu(sg) * su
        shared_out = jnp.einsum('bem,emh->beh', sh, shared_down_w).sum(axis=1)
        return (combined + shared_out).reshape(B0, S0, H0)
    h = _L0_tok_ref(x, L0_tok_w, L0_tok_b, L0_tok_cls_token, L0_tok_pos, 16)
    h = h + _L0_attn_ref(_layernorm(h, axis=-1), L0_attn_time_decay, L0_attn_time_first, L0_attn_time_mix_k, L0_attn_time_mix_v, L0_attn_time_mix_r, L0_attn_W_key, L0_attn_W_value, L0_attn_W_receptance, L0_attn_W_output)
    h = h + _L0_ffn_ref(_layernorm(h, axis=-1), L0_ffn_gate_w, L0_ffn_beta, L0_ffn_gate_proj_w, L0_ffn_up_proj_w, L0_ffn_down_proj_w, L0_ffn_shared_gate_w, L0_ffn_shared_up_w, L0_ffn_shared_down_w)
    return h

_drawn_inputs = setup_inputs


def setup_inputs(seed=0):
    import zlib

    import numpy as np

    out = dict(_drawn_inputs(seed))
    spreads = {'L0_tok_b': (0.0, 0.1), 'L0_tok_cls_token': (1.0, 0.2), 'L0_ffn_beta': (0.0, 0.534)}
    factors = {'L0_attn_time_first': 4.427,
     'L0_attn_time_mix_k': 3.905,
     'L0_attn_time_mix_r': 7.039,
     'L0_ffn_gate_w': 2.818}
    for name, (base, spread) in spreads.items():
        noise = np.random.default_rng([zlib.crc32(name.encode()), seed]).standard_normal(out[name].shape)
        drawn = base * np.exp(spread * noise) if base else spread * noise
        out[name] = jnp.asarray(drawn.astype(out[name].dtype))
    for name, factor in factors.items():
        out[name] = (out[name] * factor).astype(out[name].dtype)
    return out
```

```python
from contextlib import ExitStack, contextmanager

import numpy as np

import concourse.bass as bass
from concourse import mybir

ALU = mybir.AluOpType
ACT = mybir.ActivationFunctionType
AX = mybir.AxisListType
F32 = mybir.dt.float32
F32R = mybir.dt.float32r
F16 = mybir.dt.float16
I32 = mybir.dt.int32

P = 128
NB = 64
GRID = 6
PATCH = 16
NPATCH = GRID * GRID
T = NPATCH + 1
S = T + 1
N = NB * S
NT = N // P
C = 256
KC = C // P
F = 3 * PATCH * PATCH
FK = 7
FP = 116
CH = 8
CW = CH * S
NC = NB // CH
E = 8
NE = E + 1
M = 512
MC = M // P
TOPK = 2
RT = (TOPK * N) // P + E - 1
SH0 = 10
R0 = SH0
R1 = SH0 + RT
NF = NT + RT
EARLY = 6
LATE_AT = 3
LATE_D_AT = 9
LARGEST_AT = (12, 24, 35)
SUM_AT = R1 + 4
EPS = 1e-5
NEG = -1e38
XSCALE = 256.0
SCALED = 14
CONSTS = 3 * P + E + NT * E + RT * E
MAGIC = 8388608.0

assert R0 % 2 == 0 and R1 % 2 == 1 and N % P == 0 and NB % CH == 0 and FK * FP >= F + T + 2 and (NT - 1) % 3 == 0 and (NT - 1) // 3 == EARLY


@contextmanager
def in_steps(engine, first, end, step):
    assert first % step == 0 and end % step == 0
    with engine.Fori(first // step, end // step) as n:
        yield n * step


def wait_apart(engine, sem, value, passed):
    engine.wait_ge(sem, value)
    engine.sem_inc(passed, 1)


class Count:

    def __init__(self, sem):
        self.sem, self.at, self.n = sem, 0, 0

    def up(self, instruction):
        instruction.then_inc(self.sem, 1)
        self.at = self.at + 1
        self.n += 1
        return self.at


def vit_block(nc, x, w_tok, w_attn, chan, w_gate, beta, w_gu, w_down, consts, out):
    ctx = ExitStack()
    with ctx:
        base = (nc.sbuf_base + 31) // 32 * 32
        ctx.enter_context(nc.sbuf_tensor("arena", [P, (nc.sbuf_top - base) // 4 - 16], F32))
        top = base + ((nc.sbuf_top - base) // 4 - 16) * 4
        where = {"at": base}

        def place(name, shape, dt, at=None):
            size = int(np.prod(shape[1:])) * (2 if dt == F16 else 4)
            size = (size + 31) // 32 * 32
            if at is None:
                at = where["at"]
                where["at"] = at + size
                assert where["at"] <= top, name
            return nc.alloc_sbuf_tensor_at(name, shape, dt, offset=at), at + size

        def sem(name):
            return ctx.enter_context(nc.semaphore(name))

        WGU, _ = place("WGU", [P, NE, 2, KC, 2, M], F16)
        WD, _ = place("WD", [P, NE, 2, MC, C], F32R)
        gu_late = base + EARLY * 2 * KC * 2 * M * 2
        d_late = base + NE * 2 * KC * 2 * M * 2 + EARLY * 2 * MC * C * 4
        h_at = where["at"]
        H, h_end = place("H", [P, NT, C], F32)
        x_at = h_end
        where["at"] = h_end
        XNT, xnt_end = place("XNT", [P, KC, 1 + N], F32)
        where["at"] = xnt_end
        XS, _ = place("XS", [P, NT, 2 * C], F16)
        CH_, _ = place("CHAN", [P, 5, KC], F32)
        UV, _ = place("UV", [P, 4, KC], F32)
        GW, _ = place("GW", [P, KC, E], F32)
        BETA, _ = place("BETA", [P, E], F32)
        AM, _ = place("AM", [P, 2], F32)
        AMALL, _ = place("AMALL", [P, 2], F32)
        SBITS, _ = place("SBITS", [P, 2], I32)
        EXPO, _ = place("EXPO", [P, 2], I32)
        INV, _ = place("INV", [P, NE, 2], I32)
        EPSH, _ = place("EPSH", [P, 2], F32)
        STAT, _ = place("STAT", [P, 3, 6], F32)
        MV, _ = place("MV", [P, 3, 2], F32)
        VE, _ = place("VE", [P, 3, 1], F32)
        RSTD, _ = place("RSTD", [P, 3, 1], F32)
        LG, _ = place("LG", [P, NT, E], F32)
        POS, _ = place("POS", [P, TOPK, NT], I32)
        CW2, _ = place("CW2", [P, TOPK, NT], F32)
        EID, _ = place("EID", [1, NF], I32)
        CONST, _ = place("CONST", [P, CONSTS], F32)
        ZERO, _ = place("ZERO", [P, 2 * C], F16)
        IDENTH, _ = place("IDENTH", [P, P], F16)

        a = gu_late
        XIN, a = place("XIN", [FP, 3, FK, P], F32, a)
        WTOK, a = place("WTOK", [FP, FK, C], F32, a)
        assert a <= gu_late + 3 * 8192
        a = gu_late
        D, a = place("D", [P, KC, CW], F32, a)
        XM, a = place("XM", [P, 3, KC, CW], F32, a)
        KS, a = place("KS", [P, KC, CW], F32, a)
        VS, a = place("VS", [P, 2, KC, CW], F32, a)
        RE, a = place("RE", [P, 2, KC, CW], F32, a)
        O, a = place("O", [P, 1 + KC * CW], F32, a)
        assert a <= gu_late + 3 * 8192
        a = d_late
        XN, a = place("XN", [P, 3, C], F32, a)
        WA, a = place("WA", [P, 4, KC, C], F32, a)
        W38, a = place("W38", [P, KC, CW], F32, a)
        raw_d = a
        RN, a = place("RN", [P, 2, KC, CW], F32, a)
        NUM, a = place("NUM", [P, KC, CW], F32, a)
        ys = a
        YS, a = place("YS", [P, 3, KC, P], F32, ys)
        Q, _ = place("Q", [P, 1 + KC * CW], F32, ys)
        assert a <= d_late + 3 * 8192
        RAWD, a = place("RAWD", [P, 2, MC * C], F32, raw_d)
        assert a <= d_late + 3 * 8192
        RAWGU, a = place("RAWGU", [P, 2, 2 * KC * M], F32, xnt_end)
        assert a <= xnt_end + NT * 2 * C * 2
        a = xnt_end
        AE, a = place("AE", [P, 4, KC, CW], F32, a)
        T1, a = place("T1", [P, KC, CW], F32, a)
        DEN, a = place("DEN", [P, KC, CW], F32, a)
        PB, a = place("PB", [P, 1 + KC * CW], F32, a)
        assert a <= xnt_end + NT * 2 * C * 2
        a = gu_late
        XT3, a = place("XT3", [P, 3, KC, P], F32, a)

        a = x_at
        XR, a = place("XR", [P, 2, 2 * C], F16, a)
        XT, a = place("XT", [P, 2, 2 * KC, P], F16, a)
        ACTV, a = place("ACTV", [P, 2, M], F32, a)
        HHI, a = place("HHI", [P, 2, MC, P], F32R, a)
        HLO, a = place("HLO", [P, 2, MC, P], F32R, a)
        Y, a = place("Y", [P, 2, C], F32, a)
        assert a <= xnt_end
        a = gu_late
        R8 = [P, NT, E]
        LB, a = place("LB", R8, F32, a)
        EQ, a = place("EQ", R8, F32, a)
        OH, a = place("OH", [P, TOPK, NT, E], F32, a)
        TOT, a = place("TOT", [P, E, NT], F32, a)
        INC, a = place("INC", [P, E, NT], F32, a)
        RED, a = place("RED", [P, NT], F32, a)
        TIL, a = place("TIL", [P, 3, E], F32, a)
        GE, a = place("GE", [1, RT, E], F32, a)
        EIDF, a = place("EIDF", [1, RT], F32, a)
        LGW, a = place("LGW", [P, TOPK, NT], F32, a)
        assert a <= gu_late + 2 * KC * 2 * M * 2
        ROUTED, a = place("ROUTED", [P, TOPK, NT, C], F32, base + 2 * KC * 2 * M * 2)
        assert a <= base + NE * 2 * KC * 2 * M * 2

        half = MC * C * 4
        LATE_GU = [place(f"LATE_GU{n}", [P, 2 * KC * M], F32, at)[0]
                   for n, at in enumerate((gu_late + 2 * half, gu_late + 4 * half, d_late))]
        LATE_D = [place(f"LATE_D{n}", [P, MC * C], F32, d_late + at * half)[0] for n, at in enumerate((2, 4, 5))]

        BANK = [ctx.enter_context(nc.psum_tensor(f"bank{n}", [P, 512], F32)) for n in range(8)]
        XTURN = BANK[5][:, 0:C].bitcast(F16)

        xs_slot = nc.dram_tensor("xs_slot", [RT * P, 2 * C], F16, kind="Internal").ap()
        y_slot = nc.dram_tensor("y_slot", [RT * P, C], F32, kind="Internal").ap()

        IDENT = CONST[:, 0:P]
        TRI = CONST[:, P:2 * P]
        ONES = CONST[:, 2 * P:3 * P]
        REV = CONST[:, 3 * P:3 * P + E]
        RESET = CONST[:, 3 * P + E:3 * P + E + NT * E]
        TILES = CONST[0:1, 3 * P + E + NT * E:CONSTS].rearrange("p (j e) -> p j e", e=E)
        DECAY, FIRST, MIX = CH_[:, 0, :], CH_[:, 1, :], CH_[:, 2:5, :]
        Wv, Uv, UWv = UV[:, 0, :], CH_[:, 1, :], UV[:, 2, :]
        INVF = INV.bitcast(F32) if hasattr(INV, "bitcast") else INV[:, :, :].bitcast(F32)
        SCALE = SBITS[:, :].bitcast(F32)

        def flat(ap):
            return ap.rearrange("p k n -> p (k n)")

        def halves(bank, width):
            return bank[:, 0:2 * width].rearrange("p (k n) -> p k n", k=2)

        w_tok_loaded = sem("w_tok_loaded")
        x_loaded = [sem(f"x_loaded{u}") for u in range(3)]
        consts_loaded = sem("consts_loaded")
        small_loaded = sem("small_loaded")
        raw_loaded = sem("raw_loaded")
        consts_set = sem("consts_set")
        tok_done = sem("tok_done")
        h_ready = sem("h_ready")
        var_ready = sem("var_ready")
        rstd_ready = sem("rstd_ready")
        xn_ready = sem("xn_ready")
        xn_turned = sem("xn_turned")
        xnt_ready = sem("xnt_ready")
        am_ready = sem("am_ready")
        amall_ready = sem("amall_ready")
        scale_ready = sem("scale_ready")
        high_ready = sem("high_ready")
        low_ready = sem("low_ready")
        dlow_ready = sem("dlow_ready")
        act_passed, dve_passed, pool_passed, sp_passed = (
            sem(f"{e}_passed_wait") for e in ("scalar", "vector", "gpsimd", "sync"))
        vstep = sem("vector_step")
        astep = sem("scalar_step")
        decay_ready = sem("decay_ready")
        diff_ready = sem("diff_ready")
        mixed = sem("mixed")
        kvr_done = sem("kvr_done")
        kvr_copied = sem("kvr_copied")
        args_ready = sem("args_ready")
        exps_ready = sem("exps_ready")
        relu_ready = sem("relu_ready")
        pb_ready = sem("pb_ready")
        t1_ready = sem("t1_ready")
        bv_ready = sem("bv_ready")
        num_ready = sem("num_ready")
        den_ready = sem("den_ready")
        ln_ready = sem("ln_ready")
        s_ready = sem("s_ready")
        e_ready = sem("e_ready")
        y_ready = sem("y_ready")
        zero_stored = sem("zero_stored")
        ys_ready = sem("ys_ready")
        wo_done = sem("wo_done")
        res_ready = sem("res_ready")
        xs_ready = sem("xs_ready")
        xt3_ready = sem("xt3_ready")
        gate_done = sem("gate_done")
        logits_ready = sem("logits_ready")
        ident_ready = sem("ident_ready")
        chosen = sem("chosen")
        prefix_done = sem("prefix_done")
        tot_ready = sem("tot_ready")
        pos_ready = sem("pos_ready")
        eid_ready = sem("eid_ready")
        coef_ready = sem("coef_ready")
        scattered = sem("scattered")
        xr_loaded = [sem(f"xr_loaded{u}") for u in range(2)]
        x_turned = sem("x_turned")
        xt_ready = sem("xt_ready")
        g_done = sem("g_done")
        u_done = sem("u_done")
        silu_ready = sem("silu_ready")
        hid_ready = sem("hid_ready")
        ht_done = sem("ht_done")
        hhi_ready = sem("hhi_ready")
        hlo_ready = sem("hlo_ready")
        down_done = sem("down_done")
        y_copied = sem("y_copied")
        y_stored = [sem(f"y_stored{u}") for u in range(2)]
        late_gu = [sem(f"late_gu{n}") for n in range(NE - EARLY)]
        late_d = [sem(f"late_d{n}") for n in range(NE - EARLY)]
        gathered = [sem(f"gathered{i}") for i in range(NT)]
        summed = sem("summed")
        out_ready = sem("out_ready")
        out_stored = sem("out_stored")

        def late_raw(q):
            return LATE_GU[q - EARLY][:, :], LATE_D[q - EARLY][:, :]

        def by_part(raw_gu):
            r = raw_gu.rearrange("p (g k m) -> p g k m", g=2, k=KC)
            return [r[:, g] for g in range(2)]

        block = ctx.enter_context(nc.Block())

        @block.sync
        def _(sp):
            sp.dma_start(WTOK[:, :, :], w_tok).then_inc(w_tok_loaded, 16)
            for u in range(3):
                sp.dma_start(XIN[:, u], x[u]).then_inc(x_loaded[u], 16)

            def load_raw(q):
                if not isinstance(q, int) or q >= 1:
                    sp.wait_ge(raw_loaded, 32 * q)
                sp.dma_start(RAWGU[:, bass.ds(q % 2, 1), :].rearrange("p a n -> p (a n)"),
                             w_gu[bass.ds(q, 1)].rearrange("a p n -> (a p) n")).then_inc(raw_loaded, 16)
                sp.dma_start(RAWD[:, bass.ds(q % 2, 1), :].rearrange("p a n -> p (a n)"),
                             w_down[bass.ds(q, 1)].rearrange("a p n -> (a p) n")).then_inc(raw_loaded, 16)

            def load_tiles(q):
                for u in range(3):
                    sp.wait_ge(tok_done, 3 * q + u - 2)
                    sp.dma_start(XIN[:, u], x[bass.ds(3 * q + u, 1)].rearrange("a p f n -> (a p) f n"))\
                      .then_inc(x_loaded[u], 16)

            load_raw(0)
            load_tiles(1)
            load_raw(1)
            with sp.Fori(2, EARLY) as q:
                load_tiles(q)
                wait_apart(sp, low_ready, q - 1, sp_passed)
                wait_apart(sp, dlow_ready, q - 1, sp_passed)
                load_raw(q)
            sp.wait_ge(tok_done, NT - 3)
            sp.dma_start(XIN[:, 0], x[NT - 1]).then_inc(x_loaded[0], 16)
            sp.wait_ge(consts_set, 1)
            sp.dma_start(xs_slot.rearrange("(t p) n -> p t n", p=P),
                         ZERO[:, :].rearrange("p (a n) -> p a n", a=1).broadcast_to([P, RT, 2 * C]))\
              .then_inc(zero_stored, 16)
            sp.wait_ge(y_ready, NC)
            for n in (0, 1):
                sp.dma_start(late_raw(EARLY + n)[0], w_gu[EARLY + n]).then_inc(late_gu[n], 16)
            sp.dma_start(late_raw(EARLY + 1)[1], w_down[EARLY + 1]).then_inc(late_d[1], 16)
            sp.wait_ge(xs_ready, 2 * NT)
            sp.wait_ge(xn_turned, 2 * NT)
            sp.dma_start(late_raw(NE - 1)[0], w_gu[NE - 1]).then_inc(late_gu[2], 16)
            for n in (0, 2):
                sp.dma_start(late_raw(EARLY + n)[1], w_down[EARLY + n]).then_inc(late_d[n], 16)

            def load_xr(j, u):
                if not isinstance(j, int) or j >= R0 + 2:
                    sp.wait_ge(x_turned, j - 1)
                sp.dma_start(XR[:, u], xs_slot[bass.ds((j - R0) * P, P), :]).then_inc(xr_loaded[u], 16)

            sp.wait_ge(scattered, 16 * TOPK * NT)
            load_xr(R0, 0)
            load_xr(R0 + 1, 1)
            with in_steps(sp, R0 + 2, R1 - 1, 2) as j:
                for u in range(2):
                    load_xr(j + u, u)
            load_xr(R1 - 1, 0)
            for i in range(NT):
                sp.wait_ge(out_ready, i + 1)
                sp.dma_start(out[i * P:(i + 1) * P, :], H[:, i, :]).then_inc(out_stored, 16)
            sp.wait_ge(out_stored, 16 * NT)

        @block.tensor
        def _(pe):
            def tok(i, u):
                pe.wait_ge(x_loaded[u], 16 * (i // 3 + 1))
                for f in range(FK):
                    last = nc.tensor.matmul(BANK[u][:, 0:C], XIN[:, u, f, :], WTOK[:, f, :],
                                            start=f == 0, stop=f == FK - 1)
                last.then_inc(tok_done, 1)

            def turn(i, u, count):
                pe.wait_ge(xn_ready, count + 1)
                for k in range(KC):
                    last = nc.tensor.transpose(BANK[3 + u][:, k * P:(k + 1) * P], XN[:, u, k * P:(k + 1) * P], IDENT)
                last.then_inc(xn_turned, 1)

            pe.wait_ge(w_tok_loaded, 16)
            tok(0, 0)
            tok(1, 1)
            pe.wait_ge(consts_loaded, 16 * 4)
            with in_steps(pe, 0, NT - 4, 3) as b:
                for u in range(3):
                    tok(b + (u + 2), (u + 2) % 3)
                    turn(b + u, u, b + u)
            for i in range(NT - 4, NT):
                if i + 2 < NT:
                    tok(i + 2, (i + 2) % 3)
                turn(i, i % 3, i)
            pe.wait_ge(small_loaded, 16 * 3)

            def kvr(c):
                pe.wait_ge(xnt_ready, NT)
                for o in range(3):
                    pe.wait_ge(mixed, 3 * c + o + 1)
                    if not isinstance(c, int):
                        pe.wait_ge(kvr_copied, 3 * c)
                    for m in range(KC):
                        for k in range(KC):
                            last = nc.tensor.matmul(BANK[2 * o + m][:, 0:CW], WA[:, o, k, m * P:(m + 1) * P],
                                                    XM[:, o, k, :], start=k == 0, stop=k == KC - 1)
                    last.then_inc(kvr_done, 1)

            kvr(0)
            with pe.Fori(1, NC) as c:
                kvr(c)

            def wo(i, u):
                pe.wait_ge(ys_ready, i + 1)
                for k in range(KC):
                    last = nc.tensor.matmul(BANK[u][:, 0:C], YS[:, u, k, :], WA[:, 3, k, :], start=k == 0, stop=k == KC - 1)
                last.then_inc(wo_done, 1)

            def gate(i, u):
                pe.wait_ge(xt3_ready, i + 1)
                if not isinstance(i, int) or i >= 1:
                    pe.wait_ge(logits_ready, i)
                for k in range(KC):
                    last = nc.tensor.matmul(BANK[6][:, 0:E], XT3[:, u, k, :], GW[:, k, :], start=k == 0, stop=k == KC - 1)
                last.then_inc(gate_done, 1)

            pe.wait_ge(kvr_copied, 3 * NC)
            wo(0, 0)
            wo(1, 1)

            def token_tiles(b, end=3):
                for u in range(end):
                    i = b + u
                    if not isinstance(i, int) or i + 2 < NT:
                        wo(i + 2, (u + 2) % 3)
                    turn(i, u, i + NT)
                    if not isinstance(i, int) or i >= 1:
                        gate(i - 1, (u + 2) % 3)

            token_tiles(0)
            with in_steps(pe, 3, NT - 4, 3) as b:
                token_tiles(b)
            token_tiles(NT - 4)
            token_tiles(NT - 1, 1)
            gate(NT - 1, (NT - 1) % 3)

            def turn_x(j, u, shared):
                if shared:
                    pe.wait_ge(xs_ready, 2 * NT)
                    x = XS[:, bass.ds(j if not isinstance(j, int) or j < R0 else j - RT, 1), :]\
                        .rearrange("p a n -> p (a n)")
                else:
                    pe.wait_ge(xr_loaded[u], 8 * (j - R0 - u) + 16)
                    x = XR[:, u]
                if not isinstance(j, int) or j >= 1:
                    pe.wait_ge(xt_ready, j)
                for k in range(2 * KC):
                    last = nc.tensor.transpose(XTURN[:, k * P:(k + 1) * P], x[:, k * P:(k + 1) * P], IDENTH[:, :])
                last.then_inc(x_turned, 1)

            def gate_up(j, u, e):
                pe.wait_ge(xt_ready, j + 1)
                for g, done in ((0, g_done), (1, u_done)):
                    if not isinstance(j, int) or j >= 2:
                        pe.wait_ge((silu_ready, hid_ready)[g], j - 1)
                    n = 0
                    for k in range(KC):
                        for xh, wh in ((0, 0), (0, 1), (1, 0)):
                            w = WGU[:, bass.ds(e, 1), g, k, wh, :].rearrange("p a n -> p (a n)")
                            last = nc.tensor.matmul(BANK[2 * g + u][:, :], XT[:, u, xh * KC + k, :], w,
                                                    start=n == 0, stop=n == 3 * KC - 1)
                            n += 1
                    last.then_inc(done, 1)

            def turn_hidden(j, u):
                pe.wait_ge(hid_ready, j + 1)
                if not isinstance(j, int) or j >= 1:
                    pe.wait_ge(hlo_ready, j)
                for m in range(MC):
                    last = nc.tensor.transpose(BANK[4][:, m * P:(m + 1) * P], ACTV[:, u, m * P:(m + 1) * P], IDENT)
                last.then_inc(ht_done, 1)

            def down(j, u, e):
                pe.wait_ge(hlo_ready, j + 1)
                if not isinstance(j, int) or j >= 2:
                    pe.wait_ge(y_copied, j - 1)
                n = 0
                for m in range(MC):
                    for hid, wh in ((HHI, 0), (HHI, 1), (HLO, 0)):
                        w = WD[:, bass.ds(e, 1), wh, m, :].rearrange("p a n -> p (a n)")
                        last = nc.tensor.matmul(BANK[6 + u][:, 0:C], hid[:, u, m, :], w,
                                                start=n == 0, stop=n == 3 * MC - 1)
                        n += 1
                last.then_inc(down_done, 1)

            pe.wait_ge(logits_ready, NT)
            pe.wait_ge(ident_ready, 1)
            pe.wait_ge(low_ready, 1)
            pe.wait_ge(dlow_ready, 1)
            def feed(j, u, e, e2, turn_next):
                gate_up(j, u, e)
                if turn_next is not None:
                    turn_x(j + 1, 1 - u, turn_next)
                turn_hidden(j - 1, 1 - u)
                down(j - 2, u, e2)

            def chosen_expert(j):
                return pe.value_load(EID[0:1, bass.ds(j, 1)], min_val=0, max_val=NE - 1)

            SHARED, ROUTED_NEXT = True, False
            turn_x(0, 0, True)
            turn_x(1, 1, True)
            gate_up(0, 0, 0)
            gate_up(1, 1, 0)
            pe.wait_ge(chosen, 1)
            nc.tensor.matmul(BANK[7][:, 0:NT * E], TRI, LB[:, :, :].rearrange("p t e -> p (t e)"), start=True, stop=True)
            nc.tensor.matmul(BANK[7][:, 256:256 + NT * E], ONES, LB[:, :, :].rearrange("p t e -> p (t e)"),
                             start=True, stop=True).then_inc(prefix_done, 1)
            turn_x(2, 0, True)
            turn_hidden(0, 0)
            feed(2, 0, 0, 0, SHARED)
            pe.wait_ge(tot_ready, 1)
            feed(3, 1, 0, 0, SHARED)
            with in_steps(pe, 4, R0 - 2, 2) as j:
                for u in range(2):
                    feed(j + u, u, 0, 0, SHARED)
            feed(R0 - 2, 0, 0, 0, SHARED)
            feed(R0 - 1, 1, 0, 0, ROUTED_NEXT)
            pe.wait_ge(eid_ready, 1)
            pe.wait_ge(low_ready, NE)
            feed(R0, 0, chosen_expert(R0), 0, ROUTED_NEXT)
            feed(R0 + 1, 1, chosen_expert(R0 + 1), 0, ROUTED_NEXT)
            pe.wait_ge(dlow_ready, NE)
            with in_steps(pe, R0 + 2, R1 - 1, 2) as j:
                for u in range(2):
                    feed(j + u, u, chosen_expert(j + u), chosen_expert(j + (u - 2)), ROUTED_NEXT)
            for j in (R1 - 1, R1, R1 + 1, R1 + 2):
                feed(j, j % 2, chosen_expert(j) if j < R1 else 0, chosen_expert(j - 2) if j < R1 + 2 else 0, SHARED)
            for j in range(R1 + 3, NF - 1):
                feed(j, j % 2, 0, 0, SHARED)
            feed(NF - 1, 1, 0, 0, None)
            turn_hidden(NF - 1, 1)
            down(NF - 2, 0, 0)
            down(NF - 1, 1, 0)

        @block.scalar
        def _(act):
            for dst, src in ((CONST, consts), (CH_, chan), (GW, w_gate), (BETA, beta)):
                act.dma_start(dst[tuple(slice(None) for _ in dst.shape)], src).then_inc(consts_loaded, 16)
            for o in range(0, 3):
                n = (0, 2, 3, 4)
                act.dma_start(WA[:, n[o]:n[o + 1]], w_attn[:, n[o]:n[o + 1]]).then_inc(small_loaded, 16)
            step = Count(astep)

            act.wait_ge(consts_loaded, 16 * 4)
            nc.scalar.activation(UV[:, 1, :], DECAY, ACT.Exp).then_inc(decay_ready, 1)

            def copy_h(i, u):
                act.wait_ge(tok_done, i + 1)
                nc.scalar.activation(H[:, bass.ds(i, 1), :].rearrange("p a n -> p (a n)"), BANK[u][:, 0:C], ACT.Copy)\
                  .then_inc(h_ready, 1)

            def copy_xnt(i, u):
                act.wait_ge(xn_turned, i + 1)
                nc.scalar.activation(XNT[:, :, bass.ds(i * P + 1, P)], halves(BANK[3 + u], P), ACT.Copy)\
                  .then_inc(xnt_ready, 1)

            def high_gu(q, gu):
                act.wait_ge(scale_ready, q + 1)
                for g in range(2):
                    nc.scalar.activation(WGU[:, bass.ds(q, 1), g, :, 0, :].rearrange("p a k m -> p (a k) m"),
                                         gu[g], ACT.Copy, scale=SCALE[:, g:g + 1]).then_inc(high_ready, 1)

            def high_d(q, raw):
                nc.scalar.activation(WD[:, bass.ds(q, 1), 0].rearrange("p a m n -> p (a m n)"), raw, ACT.Copy)\
                  .then_inc(high_ready, 1)

            def raw_gu(q):
                r = RAWGU[:, bass.ds(q % 2, 1), :].rearrange("p a (g k m) -> p (a g) k m", g=2, k=KC)
                return [r[:, g] for g in range(2)]

            def first_tiles(b):
                q = b // 3
                for u in range(3):
                    if not isinstance(b, int) or b + u + 2 < NT:
                        copy_h(b + (u + 2), (u + 2) % 3)
                    copy_xnt(b + u, u)
                    if u == 0:
                        wait_apart(act, raw_loaded, 32 * q + 32, act_passed)
                        high_d(q, RAWD[:, bass.ds(q % 2, 1), :].rearrange("p a n -> p (a n)"))
                    if u == 1:
                        high_gu(q, raw_gu(q))

            copy_h(0, 0)
            copy_h(1, 1)
            with in_steps(act, 0, NT - 4, 3) as b:
                first_tiles(b)
            first_tiles(NT - 4)
            copy_xnt(NT - 1, (NT - 1) % 3)

            def copy_kvr(c):
                s = c % 2
                act.wait_ge(kvr_done, 3 * c + 1)
                if not isinstance(c, int) or c >= 1:
                    act.wait_ge(args_ready, 2 * c)
                for m in range(KC):
                    i = nc.scalar.activation(KS[:, m, :], BANK[m][:, 0:CW], ACT.Copy)
                i.then_inc(kvr_copied, 1)
                act.wait_ge(kvr_done, 3 * c + 2)
                for m in range(KC):
                    i = nc.scalar.activation(VS[:, bass.ds(s, 1), m, :].rearrange("p a n -> p (a n)"),
                                             BANK[2 + m][:, 0:CW], ACT.Copy)
                i.then_inc(kvr_copied, 1)
                act.wait_ge(kvr_done, 3 * c + 3)
                for m in range(KC):
                    nc.scalar.activation(RN[:, bass.ds(s, 1), m, :].rearrange("p a n -> p (a n)"),
                                         BANK[4 + m][:, 0:CW], ACT.Relu, scale=-1.0)
                for m in range(KC):
                    i = nc.scalar.activation(RE[:, bass.ds(s, 1), m, :].rearrange("p a n -> p (a n)"),
                                             BANK[4 + m][:, 0:CW], ACT.Abs)
                i.then_inc(kvr_copied, 1)
                wait_apart(act, kvr_copied, 3 * c + 3, act_passed)
                re = RE[:, bass.ds(s, 1)].rearrange("p a k n -> p (a k n)")
                step.up(nc.scalar.activation(re, re, ACT.Exp, scale=-1.0))

            def exps(c, last):
                for n, scale in enumerate((1.0, -1.0)):
                    act.wait_ge(args_ready, 2 * c + n + 1)
                    nc.scalar.activation(flat(AE[:, n]), flat(AE[:, n]), ACT.Exp, scale=scale).then_inc(exps_ready, 1)
                if last is not None:
                    ratio(last)
                nc.scalar.activation(flat(AE[:, 2]), flat(AE[:, 3]), ACT.Relu).then_inc(relu_ready, 1)
                act.wait_ge(relu_ready, 2 * c + 1)
                nc.scalar.activation(flat(AE[:, 3]), flat(AE[:, 3]), ACT.Relu, scale=-1.0).then_inc(relu_ready, 1)
                act.wait_ge(relu_ready, 2 * c + 2)
                ae = AE[:, 2:4].rearrange("p n k m -> p (n k m)")
                nc.scalar.activation(ae, ae, ACT.Exp, scale=-1.0).then_inc(exps_ready, 1)

            def logarithm(c):
                act.wait_ge(den_ready, c + 1)
                nc.scalar.activation(flat(DEN[:, :, :]), flat(DEN[:, :, :]), ACT.Ln).then_inc(ln_ready, 1)

            def ratio(c):
                act.wait_ge(s_ready, c + 1)
                nc.scalar.activation(flat(DEN[:, :, :]), flat(DEN[:, :, :]), ACT.Exp, scale=-1.0).then_inc(e_ready, 1)

            nc.scalar.preload_act_table_set("natural_log_exp_and_others")
            copy_kvr(0)
            exps(0, None)
            copy_kvr(1)
            with act.Fori(1, NC - 1) as c:
                logarithm(c - 1)
                exps(c, c - 1)
                copy_kvr(c + 1)
            logarithm(NC - 2)
            exps(NC - 1, NC - 2)
            logarithm(NC - 1)
            ratio(NC - 1)

            def copy_ys(i, u):
                act.wait_ge(y_ready, NC)
                nc.scalar.activation(YS[:, u], XNT[:, :, bass.ds(i * P + 1, P)], ACT.Copy).then_inc(ys_ready, 1)

            def copy_xt3(i, u):
                act.wait_ge(xn_turned, i + (NT + 1))
                nc.scalar.activation(XT3[:, u], halves(BANK[3 + u], P), ACT.Copy).then_inc(xt3_ready, 1)

            def copy_logits(i):
                act.wait_ge(gate_done, i + 1)
                nc.scalar.activation(LG[:, bass.ds(i, 1), :].rearrange("p a n -> p (a n)"), BANK[6][:, 0:E], ACT.Copy)\
                  .then_inc(logits_ready, 1)

            for i in range(3):
                copy_ys(i, i)

            def token_tiles(b, end=3):
                for u in range(end):
                    i = b + u
                    if not isinstance(i, int) or i + 3 < NT:
                        act.wait_ge(wo_done, i + 1)
                        copy_ys(i + 3, u)
                    copy_xt3(i, u)
                    if not isinstance(i, int) or i >= 1:
                        copy_logits(i - 1)

            token_tiles(0)
            with in_steps(act, 3, NT - 4, 3) as b:
                token_tiles(b)
            token_tiles(NT - 4)
            token_tiles(NT - 1, 1)
            copy_logits(NT - 1)

            def silu(j, u, e):
                act.wait_ge(g_done, j + 1)
                if not isinstance(j, int) or j >= 2:
                    act.wait_ge(ht_done, j - 1)
                nc.scalar.activation(ACTV[:, u], BANK[u][:, :], ACT.Silu,
                                     scale=INVF[:, bass.ds(e, 1), 0]).then_inc(silu_ready, 1)

            def hidden_high(j, u):
                act.wait_ge(ht_done, j + 1)
                if not isinstance(j, int) or j >= 2:
                    act.wait_ge(down_done, j - 1)
                nc.scalar.activation(HHI[:, u].rearrange("p m n -> p (m n)"), BANK[4][:, :], ACT.Copy)\
                  .then_inc(hhi_ready, 1)

            def store_y(j, u):
                act.wait_ge(y_copied, j + 1)
                act.dma_start(y_slot[bass.ds((j - R0) * P, P), :], Y[:, u]).then_inc(y_stored[u], 16)

            def feed(j, u, e, store):
                silu(j, u, e)
                hidden_high(j - 1, 1 - u)
                if store:
                    store_y(j - 2, u)

            def chosen_expert(j):
                return act.value_load(EID[0:1, bass.ds(j, 1)], min_val=0, max_val=NE - 1)

            act.wait_ge(chosen, 2)
            nc.scalar.activation(CW2[:, :, :], LGW[:, :, :], ACT.Sigmoid).then_inc(coef_ready, 1)
            silu(0, 0, 0)
            for j in range(1, R0):
                feed(j, j % 2, 0, False)
                n, part = divmod(j - LATE_AT, 2)
                if 0 <= n < NE - EARLY and part == 1:
                    high_gu(EARLY + n, by_part(late_raw(EARLY + n)[0]))
                if j == LATE_D_AT:
                    for n in range(NE - EARLY):
                        act.wait_ge(late_d[n], 16)
                        if n == 0:
                            act.wait_ge(low_ready, NE)
                        else:
                            act.wait_ge(dlow_ready, EARLY + n)
                        high_d(EARLY + n, late_raw(EARLY + n)[1])
            act.wait_ge(eid_ready, 1)
            for u in range(2):
                feed(R0 + u, u, chosen_expert(R0 + u), False)
            with in_steps(act, R0 + 2, R1 + 1, 2) as j:
                for u in range(2):
                    feed(j + u, u, chosen_expert(j + u), True)
            feed(R1 + 1, 0, 0, True)
            feed(R1 + 2, 1, 0, False)
            with in_steps(act, R1 + 3, NF, 2) as j:
                for u in range(2):
                    feed(j + u, u, 0, False)
            hidden_high(NF - 1, 1)

        @block.vector
        def _(dve):
            step = Count(vstep)

            def then(mark):
                dve.wait_ge(vstep, mark)

            def after(instruction):
                then(step.up(instruction))

            step.up(nc.vector.memset(XNT[:, :, 0:1], 0.0))
            step.up(nc.vector.memset(W38[:, :, :], 0.0))
            step.up(nc.vector.memset(EID[:, :], 0))
            nc.vector.memset(EPSH[:, 1:2], -0.5).then_inc(var_ready, 1)
            dve.wait_ge(decay_ready, 1)
            after(nc.vector.tensor_scalar(Wv, UV[:, 1, :], -1.0, None, ALU.mult))
            step.up(nc.vector.tensor_tensor(UWv, Uv, Wv, ALU.add))
            for k in range(KC):
                after(nc.vector.tensor_scalar(W38[:, k, :], W38[:, k, :], Wv[:, k:k + 1], None, ALU.add))
            after(nc.vector.memset(W38[:, :, :].rearrange("p k (b s) -> p k b s", s=S)[:, :, :, 0], 2 * NEG))

            def tile_of(i):
                return H[:, bass.ds(i, 1), :].rearrange("p a n -> p (a n)")

            def stats(i, u):
                return step.up(nc.vector.bn_stats(STAT[:, u], tile_of(i)))

            def variance(u, mark):
                wait_apart(dve, vstep, mark, dve_passed)
                return step.up(nc.vector.bn_aggr(MV[:, u], STAT[:, u]))

            def var_eps(u, mark):
                then(mark)
                nc.vector.tensor_scalar(VE[:, u], MV[:, u, 1:2], EPS, None, ALU.add).then_inc(var_ready, 1)

            def affine(i, u, count):
                dve.wait_ge(rstd_ready, count + 1)
                nc.vector.tensor_scalar(XN[:, u], tile_of(i), MV[:, u, 0:1], RSTD[:, u], ALU.subtract, ALU.mult)\
                  .then_inc(xn_ready, 1)

            def largest(q, gu):
                nc.vector.tensor_reduce(AM[:, :], gu, AX.X, ALU.max,
                                        apply_absolute_value=True).then_inc(am_ready, 1)

            def scales(q):
                dve.wait_ge(amall_ready, q + 1)
                after(nc.vector.tensor_scalar(EXPO[:, :], AMALL[:, :].bitcast(I32), 0x7F800000, None, ALU.bitwise_and))
                inv = INV[:, bass.ds(q, 1), :].rearrange("p a n -> p (a n)")
                after(nc.vector.tensor_scalar(inv, EXPO[:, :], float(30 << 23), float((SCALED + 8) << 23),
                                              ALU.max, ALU.subtract))
                nc.vector.tensor_scalar(SBITS[:, :], inv, -1.0, float(246 << 23), ALU.mult, ALU.add)\
                  .then_inc(scale_ready, 1)

            def split_low(q, gu, high):
                dve.wait_ge(scale_ready, q + 1)
                for g in range(2):
                    dve.wait_ge(high_ready, high + (g + 1))
                    w = WGU[:, bass.ds(q, 1), g].rearrange("p a k h m -> p (a k) h m")
                    last = nc.vector.scalar_tensor_tensor(w[:, :, 1], gu[g], SCALE[:, g:g + 1], w[:, :, 0],
                                                          ALU.mult, ALU.subtract)
                last.then_inc(low_ready, 1)

            def raw_gu(q):
                r = RAWGU[:, bass.ds(q % 2, 1), :].rearrange("p a (g k m) -> p (a g) k m", g=2, k=KC)
                return [r[:, g] for g in range(2)]

            dve.wait_ge(h_ready, 1)
            var_eps(0, variance(0, stats(0, 0)))
            start = step.at
            with in_steps(dve, 0, NT - 1, 3) as b:
                q = b // 3
                step.at = start + q * 8
                n0 = step.n
                for u in range(3):
                    n = (u + 1) % 3
                    dve.wait_ge(h_ready, b + (u + 2))
                    mark = stats(b + (u + 1), n)
                    affine(b + u, u, b + u)
                    var_eps(n, variance(n, mark))
                    if u == 0:
                        wait_apart(dve, raw_loaded, 32 * q + 32, dve_passed)
                        largest(q, RAWGU[:, bass.ds(q % 2, 1), :].rearrange("p a (g n) -> p (a g) n", g=2))
                    if u == 1:
                        scales(q)
                    if u == 2:
                        split_low(q, raw_gu(q), 3 * q + 1)
                assert step.n - n0 == 8
            step.at = start + EARLY * 8
            affine(NT - 1, 0, NT - 1)

            nc.vector.tensor_copy(IDENTH[:, :], IDENT).then_inc(ident_ready, 1)
            dve.wait_ge(low_ready, EARLY)
            dve.wait_ge(dlow_ready, EARLY)
            step.up(nc.vector.memset(O[:, 0:1], NEG))
            step.up(nc.vector.memset(PB[:, 0:1], 0.0))
            after(nc.vector.memset(Q[:, 0:1], 0.0))
            dve.wait_ge(xnt_ready, NT)
            dve.wait_ge(tok_done, NT)

            def mix(c):
                dve.wait_ge(diff_ready, c + 1)
                xx = XNT[:, :, bass.ds(c * CW, CW)]
                for o in range(3):
                    if not isinstance(c, int) or c >= 1:
                        dve.wait_ge(kvr_done, 3 * c - 2 + o)
                    for k in range(KC):
                        i = nc.vector.scalar_tensor_tensor(XM[:, o, k, :], D[:, k, :], MIX[:, o, k:k + 1], xx[:, k, :],
                                                           ALU.mult, ALU.add)
                    i.then_inc(mixed, 1)

            def scan_max(c):
                dve.wait_ge(kvr_copied, 3 * c + 1)
                after(nc.vector.memset(KS[:, :, :].rearrange("p k (b s) -> p k b s", s=S)[:, :, :, 0], NEG))
                after(nc.vector.tensor_tensor_scan(O[:, 1:], flat(W38[:, :, :]), flat(KS[:, :, :]), NEG, ALU.add, ALU.max))
                if not isinstance(c, int) or c >= 1:
                    dve.wait_ge(t1_ready, c)
                for k in range(KC):
                    i = nc.vector.scalar_tensor_tensor(AE[:, 3, k, :], O[:, k * CW:(k + 1) * CW], Uv[:, k:k + 1],
                                                       KS[:, k, :], ALU.subtract, ALU.subtract)
                    step.up(i)
                then(step.at)
                for n, op in ((0, ALU.min), (1, ALU.max)):
                    for k in range(KC):
                        i = nc.vector.tensor_scalar(AE[:, n, k, :], AE[:, 3, k, :], UWv[:, k:k + 1], 0.0, ALU.add, op)
                    i.then_inc(args_ready, 1)

            def scan_sums(c):
                dve.wait_ge(exps_ready, 3 * c + 2)
                a2, b2, bb, aa = (flat(AE[:, n]) for n in range(4))
                step.up(nc.vector.tensor_tensor_scan(Q[:, 1:], a2, b2, 0.0, ALU.mult, ALU.add))
                q_mark = step.at
                dve.wait_ge(kvr_copied, 3 * c + 2)
                vs = VS[:, bass.ds(c % 2, 1)].rearrange("p a k n -> p (a k n)")
                then(q_mark)
                after(nc.vector.tensor_tensor(b2, b2, vs, ALU.mult))
                nc.vector.tensor_tensor_scan(PB[:, 1:], a2, b2, 0.0, ALU.mult, ALU.add).then_inc(pb_ready, 1)
                dve.wait_ge(exps_ready, 3 * c + 3)
                after(nc.vector.tensor_tensor(flat(DEN[:, :, :]), aa, Q[:, 0:KC * CW], ALU.mult))
                after(nc.vector.tensor_tensor(flat(DEN[:, :, :]), flat(DEN[:, :, :]), bb, ALU.add))
                dve.wait_ge(astep, c + 1)
                nc.vector.scalar_tensor_tensor(flat(DEN[:, :, :]), RE[:, bass.ds(c % 2, 1)].rearrange("p a k n -> p (a k n)"),
                                               1.0, flat(DEN[:, :, :]), ALU.add, ALU.mult).then_inc(den_ready, 1)

            def finish(c):
                dve.wait_ge(e_ready, c + 1)
                dve.wait_ge(num_ready, c + 1)
                nc.vector.tensor_tensor(XNT[:, :, bass.ds(c * CW + 1, CW)], NUM[:, :, :], DEN[:, :, :], ALU.mult)\
                  .then_inc(y_ready, 1)

            PER = 8
            start = step.at
            mix(0)
            n0 = step.n
            scan_max(0)
            mix(1)
            scan_sums(0)
            assert step.n - n0 == PER, step.n - n0
            with dve.Fori(1, NC - 1) as c:
                step.at = start + PER * c
                scan_max(c)
                mix(c + 1)
                finish(c - 1)
                scan_sums(c)
            step.at = start + PER * (NC - 1)
            scan_max(NC - 1)
            finish(NC - 2)
            scan_sums(NC - 1)
            finish(NC - 1)

            def residual(i, u):
                dve.wait_ge(wo_done, i + 1)
                nc.vector.tensor_tensor(tile_of(i), BANK[u][:, 0:C], tile_of(i), ALU.add).then_inc(res_ready, 1)

            def out_stats(i, u):
                wait_apart(dve, res_ready, i + 1, dve_passed)
                return stats(i, u)

            def parts(i, u, part):
                xs = XS[:, bass.ds(i, 1), :].rearrange("p a (h n) -> p (a h) n", h=2)
                if part == 0:
                    dve.wait_ge(xn_ready, i + NT + 1)
                    nc.vector.tensor_scalar(xs[:, 0], XN[:, u], XSCALE, None, ALU.mult).then_inc(xs_ready, 1)
                else:
                    dve.wait_ge(xs_ready, 2 * i + 1)
                    nc.vector.scalar_tensor_tensor(xs[:, 1], XN[:, u], XSCALE, xs[:, 0], ALU.mult, ALU.subtract)\
                      .then_inc(xs_ready, 1)

            residual(0, 0)
            var_eps(0, variance(0, out_stats(0, 0)))
            start = step.at
            with in_steps(dve, 0, NT - 1, 3) as b:
                for u in range(3):
                    step.at = start + b * 2 + 2 * u
                    n = (u + 1) % 3
                    residual(b + (u + 1), n)
                    affine(b + u, u, b + (NT + u))
                    mark = out_stats(b + (u + 1), n)
                    parts(b + u, u, 0)
                    mark = variance(n, mark)
                    parts(b + u, u, 1)
                    var_eps(n, mark)
            step.at = start + 2 * (NT - 1)
            affine(NT - 1, 0, 2 * NT - 1)
            parts(NT - 1, 0, 0)
            parts(NT - 1, 0, 1)

            def copy_xt(j, u):
                dve.wait_ge(x_turned, j + 1)
                if not isinstance(j, int) or j >= 2:
                    dve.wait_ge(u_done, j - 1)
                nc.vector.tensor_copy(XT[:, u].rearrange("p k n -> p (k n)"), XTURN).then_inc(xt_ready, 1)

            def hidden(j, u, e):
                dve.wait_ge(silu_ready, j + 1)
                dve.wait_ge(u_done, j + 1)
                nc.vector.scalar_tensor_tensor(ACTV[:, u], BANK[2 + u][:, :], INVF[:, bass.ds(e, 1), 1], ACTV[:, u],
                                               ALU.mult, ALU.mult).then_inc(hid_ready, 1)

            def hidden_low(j, u):
                dve.wait_ge(hhi_ready, j + 1)
                nc.vector.tensor_tensor(HLO[:, u].rearrange("p m n -> p (m n)"), BANK[4][:, :],
                                        HHI[:, u].rearrange("p m n -> p (m n)"), ALU.subtract).then_inc(hlo_ready, 1)

            copy_xt(0, 0)
            copy_xt(1, 1)
            dve.wait_ge(logits_ready, NT)
            rev = REV.rearrange("p (a e) -> p a e", a=1).broadcast_to(R8)

            def over_e(ap):
                return ap.rearrange("p (t a) -> p t a", a=1).broadcast_to(R8)

            after(nc.vector.tensor_tensor(LB[:, :, :], LG[:, :, :],
                                          BETA[:, :].rearrange("p (a e) -> p a e", a=1).broadcast_to(R8), ALU.add))
            for w in range(TOPK):
                after(nc.vector.tensor_reduce(RED[:, :], LB[:, :, :], AX.X, ALU.max))
                after(nc.vector.tensor_tensor(EQ[:, :, :], LB[:, :, :], over_e(RED[:, :]), ALU.is_equal))
                after(nc.vector.tensor_tensor(EQ[:, :, :], EQ[:, :, :], rev, ALU.mult))
                after(nc.vector.tensor_reduce(RED[:, :], EQ[:, :, :], AX.X, ALU.max))
                after(nc.vector.tensor_tensor(OH[:, w], EQ[:, :, :], over_e(RED[:, :]), ALU.is_equal))
                if w == 0:
                    after(nc.vector.scalar_tensor_tensor(LB[:, :, :], OH[:, 0], NEG, LB[:, :, :], ALU.mult, ALU.add))
            nc.vector.tensor_tensor(LB[:, :, :], OH[:, 0], OH[:, 1], ALU.add).then_inc(chosen, 1)
            for w in range(TOPK):
                after(nc.vector.tensor_tensor(EQ[:, :, :], OH[:, w], LG[:, :, :], ALU.mult))
                i = nc.vector.tensor_reduce(LGW[:, w], EQ[:, :, :], AX.X, ALU.add)
                if w == 0:
                    after(i)
                else:
                    i.then_inc(chosen, 1)

            def late_down_low(q):
                dve.wait_ge(high_ready, 2 * NE + q + 1)
                nc.vector.tensor_tensor(WD[:, q, 1].rearrange("p m n -> p (m n)"), late_raw(q)[1],
                                        WD[:, q, 0].rearrange("p m n -> p (m n)").bitcast(F32), ALU.subtract)\
                  .then_inc(dlow_ready, 1)

            def add_y(j, u):
                dve.wait_ge(down_done, j + 1)
                i = j if j < R0 else j - RT
                nc.vector.tensor_tensor(H[:, i], BANK[6 + u][:, 0:C], H[:, i], ALU.add).then_inc(y_copied, 1)

            def copy_y(j, u):
                dve.wait_ge(down_done, j + 1)
                if not isinstance(j, int) or j >= R0 + 2:
                    dve.wait_ge(y_stored[u], 8 * (j - R0 - u))
                nc.vector.tensor_copy(Y[:, u], BANK[6 + u][:, 0:C]).then_inc(y_copied, 1)

            def feed(j, u, e, out_y, copy_next=True):
                hidden(j, u, e)
                if copy_next:
                    copy_xt(j + 1, 1 - u)
                hidden_low(j - 1, 1 - u)
                out_y(j - 2, u)

            hidden(0, 0, 0)
            copy_xt(2, 0)
            hidden_low(0, 0)
            hidden(1, 1, 0)
            dve.wait_ge(prefix_done, 1)
            dve.wait_ge(chosen, 2)
            after(nc.vector.tensor_copy(TOT[:, :, :], BANK[7][:, 256:256 + NT * E].rearrange("p (t e) -> p e t", e=E)))
            after(nc.vector.tensor_tensor_scan(INC[:, :, :].rearrange("p e t -> p (e t)"), RESET,
                                               TOT[:, :, :].rearrange("p e t -> p (e t)"), 0.0, ALU.mult, ALU.add))
            after(nc.vector.tensor_scalar(TIL[:, 0], INC[:, :, NT - 1], 1.0 / P, 0.5 - 0.25 / P, ALU.mult, ALU.add))
            after(nc.vector.tensor_scalar(TIL[:, 0], TIL[:, 0], MAGIC, MAGIC, ALU.add, ALU.subtract))
            after(nc.vector.tensor_tensor_scan(TIL[:, 1], ONES[:, 0:E], TIL[:, 0], 0.0, ALU.mult, ALU.add))
            after(nc.vector.tensor_tensor(TIL[:, 2], TIL[:, 1], TIL[:, 0], ALU.subtract))
            after(nc.vector.tensor_tensor(GE[:, :, :], TILES,
                                          TIL[0:1, 1].rearrange("p (a e) -> p a e", a=1).broadcast_to([1, RT, E]), ALU.is_ge))
            after(nc.vector.tensor_reduce(EIDF[:, :], GE[:, :, 0:E - 1], AX.X, ALU.add))
            nc.vector.tensor_scalar(EID[:, R0:R1], EIDF[:, :], 1.0, None, ALU.add).then_inc(eid_ready, 1)
            after(nc.vector.tensor_scalar(TIL[:, 2], TIL[:, 2], float(P), None, ALU.mult))
            after(nc.vector.tensor_tensor(INC[:, :, :], INC[:, :, :], TOT[:, :, :], ALU.subtract))
            after(nc.vector.tensor_tensor(INC[:, :, :], INC[:, :, :],
                                          TIL[:, 2].rearrange("p (e a) -> p e a", a=1).broadcast_to([P, E, NT]), ALU.add))
            after(nc.vector.tensor_tensor(LB[:, :, :], INC[:, :, :].rearrange("p e t -> p t e"),
                                          BANK[7][:, 0:NT * E].rearrange("p (t e) -> p t e", e=E), ALU.add))
            for w in range(TOPK):
                after(nc.vector.tensor_tensor(EQ[:, :, :], OH[:, w], LB[:, :, :], ALU.mult))
                after(nc.vector.tensor_reduce(RED[:, :], EQ[:, :, :], AX.X, ALU.add))
                nc.vector.tensor_copy(POS[:, w], RED[:, :]).then_inc(pos_ready, 1)
                dve.wait_ge(pos_ready, w + 1)
            nc.vector.engine_nop().then_inc(tot_ready, 1)

            for j in range(2, R0):
                feed(j, j % 2, 0, add_y, copy_next=j + 1 < R0)
                n, part = divmod(j - LATE_AT, 2)
                if part == 0 and 0 < n <= NE - EARLY:
                    split_low(EARLY + n - 1, by_part(late_raw(EARLY + n - 1)[0]), 3 * EARLY + 2 * (n - 1))
                if part == 0 and 0 <= n < NE - EARLY:
                    dve.wait_ge(late_gu[n], 16)
                    largest(EARLY + n, late_raw(EARLY + n)[0].rearrange("p (g n) -> p g n", g=2))
                if part == 1 and 0 <= n < NE - EARLY:
                    scales(EARLY + n)
                if j == LATE_D_AT:
                    for n in range(NE - EARLY):
                        late_down_low(EARLY + n)

            copy_xt(R0, 0)
            for j in range(R0, R0 + 4):
                e = dve.value_load(EID[0:1, j:j + 1], min_val=0, max_val=NE - 1)
                feed(j, j % 2, e, add_y if j < R0 + 2 else copy_y)
            with in_steps(dve, R0 + 4, R1 - 1, 2) as j:
                for u in range(2):
                    e = dve.value_load(EID[0:1, bass.ds(j + u, 1)], min_val=0, max_val=NE - 1)
                    feed(j + u, u, e, copy_y)
            e = dve.value_load(EID[0:1, R1 - 1:R1], min_val=0, max_val=NE - 1)
            feed(R1 - 1, 0, e, copy_y)

            mark = Count(summed)

            def add_routed(first, end):
                for w in range(TOPK):
                    for i in range(first, end):
                        if w == 0:
                            dve.wait_ge(gathered[i], 16 * TOPK)
                            dve.wait_ge(y_copied, i + 1 if i < SH0 else i + RT + 1)
                        done = nc.vector.scalar_tensor_tensor(H[:, i], ROUTED[:, w, i], CW2[:, w, i:i + 1],
                                                              H[:, i], ALU.mult, ALU.add)
                        if w == TOPK - 1:
                            done.then_inc(out_ready, 1)
                        else:
                            mark.up(done)
                    if w == 0:
                        dve.wait_ge(summed, mark.n)

            dve.wait_ge(coef_ready, 1)
            at = 0
            for j in range(R1, NF):
                feed(j, j % 2, 0, copy_y if j < R1 + 2 else add_y, copy_next=j + 1 < NF)
                if j >= SUM_AT:
                    add_routed(at, at + 2)
                    at += 2
            hidden_low(NF - 1, 1)
            add_y(NF - 2, 0)
            add_y(NF - 1, 1)
            assert at <= NT - 2
            while at < NT:
                add_routed(at, min(at + 2, NT))
                at += 2

        @block.gpsimd
        def _(pool):
            nc.gpsimd.memset(ZERO[:, :], 0.0).then_inc(consts_set, 1)

            def inv_sqrt(u, count):
                pool.wait_ge(var_ready, count + 2)
                nc.gpsimd.tensor_tensor(RSTD[:, u], VE[:, u], EPSH[:, 1:2], ALU.pow).then_inc(rstd_ready, 1)

            def all_largest(q):
                wait_apart(pool, am_ready, q + 1, pool_passed)
                nc.gpsimd.partition_all_reduce(AMALL[:, :], AM[:, :], P,
                                               bass.bass_isa.ReduceOp.max).then_inc(amall_ready, 1)

            def split_down_low(q, raw):
                pool.wait_ge(high_ready, 3 * q + 1)
                w = WD[:, bass.ds(q, 1)].rearrange("p a h m n -> p (a h) (m n)")
                nc.gpsimd.tensor_tensor(w[:, 1], raw, w[:, 0].bitcast(F32), ALU.subtract).then_inc(dlow_ready, 1)

            inv_sqrt(0, 0)
            with in_steps(pool, 0, NT - 1, 3) as b:
                q = b // 3
                inv_sqrt(1, b + 1)
                all_largest(q)
                inv_sqrt(2, b + 2)
                split_down_low(q, RAWD[:, bass.ds(q % 2, 1), :].rearrange("p a n -> p (a n)"))
                inv_sqrt(0, b + 3)
            pool.wait_ge(xnt_ready, NT)

            def diff(c):
                if not isinstance(c, int) or c >= 1:
                    pool.wait_ge(mixed, 3 * c)
                nc.gpsimd.tensor_tensor(D[:, :, :], XNT[:, :, bass.ds(c * CW + 1, CW)], XNT[:, :, bass.ds(c * CW, CW)],
                                        ALU.subtract).then_inc(diff_ready, 1)

            def numerator(c):
                pool.wait_ge(exps_ready, 3 * c + 3)
                pool.wait_ge(kvr_copied, 3 * c + 2)
                if not isinstance(c, int) or c >= 1:
                    pool.wait_ge(y_ready, c)
                vs = VS[:, bass.ds(c % 2, 1)].rearrange("p a k n -> p (a k n)")
                nc.gpsimd.tensor_tensor(flat(NUM[:, :, :]), flat(AE[:, 2]), vs, ALU.mult).then_inc(bv_ready, 1)
                pool.wait_ge(pb_ready, c + 1)
                nc.gpsimd.tensor_tensor(flat(T1[:, :, :]), flat(AE[:, 3]), PB[:, 0:KC * CW], ALU.mult)\
                  .then_inc(t1_ready, 1)
                pool.wait_ge(bv_ready, c + 1)
                pool.wait_ge(t1_ready, c + 1)
                nc.gpsimd.tensor_tensor(flat(NUM[:, :, :]), flat(NUM[:, :, :]), flat(T1[:, :, :]), ALU.add)\
                  .then_inc(num_ready, 1)

            def add_negative(c):
                pool.wait_ge(ln_ready, c + 1)
                nc.gpsimd.tensor_tensor(flat(DEN[:, :, :]), flat(DEN[:, :, :]),
                                        RN[:, bass.ds(c % 2, 1)].rearrange("p a k n -> p (a k n)"), ALU.add)\
                  .then_inc(s_ready, 1)

            pool.wait_ge(tok_done, NT)
            diff(0)
            diff(1)

            def chunk(c):
                numerator(c)
                if not isinstance(c, int) or c + 2 < NC:
                    diff(c + 2)
                add_negative(c)

            chunk(0)
            with pool.Fori(1, NC - 2) as c:
                chunk(c)
            chunk(NC - 2)
            chunk(NC - 1)

            with in_steps(pool, 0, NT - 1, 3) as b:
                for u in range(3):
                    inv_sqrt(u, b + (NT + u))
            inv_sqrt(0, 2 * NT - 1)

            pool.wait_ge(zero_stored, 16)
            for n, (w, i) in enumerate((w, i) for w in range(TOPK) for i in range(NT)):
                pool.wait_ge(pos_ready, w + 1)
                if n in LARGEST_AT:
                    all_largest(EARLY + LARGEST_AT.index(n))
                nc.gpsimd.indirect_dma_start(
                    out=xs_slot, out_offset=bass.IndirectOffsetOnAxis(ap=POS[:, w, i:i + 1], axis=0),
                    in_=XS[:, i, :], in_offset=None).then_inc(scattered, 16)

            pool.wait_ge(scattered, 16 * TOPK * NT)
            for u in range(2):
                pool.wait_ge(y_stored[u], 16 * len(range(R0 + u, R1, 2)))
            for i in range(NT):
                for w in range(TOPK):
                    nc.gpsimd.indirect_dma_start(
                        out=ROUTED[:, w, i, :], out_offset=None, in_=y_slot,
                        in_offset=bass.IndirectOffsetOnAxis(ap=POS[:, w, i:i + 1], axis=0)).then_inc(gathered[i], 16)


_ORDER = ("x", "w_tok", "w_attn", "chan", "w_gate", "beta", "w_gu", "w_down", "consts")


def build(nc, arrays):
    aps = [nc.dram_tensor(f"in_{n}", arrays[n].shape, mybir.dt.from_np(arrays[n].dtype), kind="ExternalInput").ap()
           for n in _ORDER]
    out = nc.dram_tensor("out_0", (N, C), F32, kind="ExternalOutput").ap()
    vit_block(nc, *aps, out)


def shape_constants():
    c = np.zeros((P, CONSTS), np.float32)
    c[:, 0:P] = np.eye(P)
    c[:, P:2 * P] = np.triu(np.ones((P, P)), 1)
    c[:, 2 * P:3 * P] = 1.0
    c[:, 3 * P:3 * P + E] = E - np.arange(E)
    c[:, 3 * P + E:3 * P + E + NT * E] = np.arange(NT * E) % NT != 0
    c[:, 3 * P + E + NT * E:] = np.repeat(np.arange(RT), E)
    return c


def lay_out(x, L0_tok_w, L0_tok_b, L0_tok_cls_token, L0_tok_pos, L0_attn_time_decay, L0_attn_time_first,
            L0_attn_time_mix_k, L0_attn_time_mix_v, L0_attn_time_mix_r, L0_attn_W_key, L0_attn_W_value,
            L0_attn_W_receptance, L0_attn_W_output, L0_ffn_gate_w, L0_ffn_beta, L0_ffn_gate_proj_w,
            L0_ffn_up_proj_w, L0_ffn_down_proj_w, L0_ffn_shared_gate_w, L0_ffn_shared_up_w, L0_ffn_shared_down_w):
    f32 = np.float32
    cols = np.zeros((FK * FP, NB, S), f32)
    patches = np.asarray(x).reshape(NB, 3, GRID, PATCH, GRID, PATCH).transpose(1, 3, 5, 0, 2, 4)
    cols[0:F, :, 2:] = patches.reshape(F, NB, NPATCH)
    for t in range(T):
        cols[F + t, :, t + 1] = 1.0
    cols[F + T, :, 2:] = 1.0
    cols[F + T + 1, :, 1] = 1.0
    rows = np.zeros((FK * FP, C), f32)
    rows[0:F] = np.asarray(L0_tok_w).T
    rows[F:F + T] = L0_tok_pos
    rows[F + T] = L0_tok_b
    rows[F + T + 1] = L0_tok_cls_token

    def by_partition(a, *tail):
        a = np.asarray(a)
        return a.reshape(-1, P, *a.shape[1:]).swapaxes(0, 1)

    chan = [np.asarray(v).reshape(C) for v in (L0_attn_time_decay, L0_attn_time_first, L0_attn_time_mix_k,
                                               L0_attn_time_mix_v, L0_attn_time_mix_r)]
    attn = [np.asarray(w).T for w in (L0_attn_W_key, L0_attn_W_value, L0_attn_W_receptance, L0_attn_W_output)]
    gates = np.concatenate([L0_ffn_shared_gate_w, L0_ffn_gate_proj_w])
    ups = np.concatenate([L0_ffn_shared_up_w, L0_ffn_up_proj_w])
    downs = np.concatenate([L0_ffn_shared_down_w, L0_ffn_down_proj_w])
    gu = np.stack([gates, ups], 1).reshape(NE, 2, KC, P, M).transpose(0, 3, 1, 2, 4)
    arrays = {
        "x": cols.reshape(FK, FP, NT, P).transpose(2, 1, 0, 3),
        "w_tok": rows.reshape(FK, FP, C).transpose(1, 0, 2),
        "w_attn": np.stack([by_partition(w) for w in attn], 1),
        "chan": np.stack([by_partition(v) for v in chan], 1),
        "w_gate": by_partition(np.asarray(L0_ffn_gate_w).T),
        "beta": np.broadcast_to(np.asarray(L0_ffn_beta), (P, E)),
        "w_gu": gu.reshape(NE, P, 2 * KC * M),
        "w_down": downs.reshape(NE, MC, P, C).transpose(0, 2, 1, 3).reshape(NE, P, MC * C),
        "consts": shape_constants(),
    }
    return {k: np.ascontiguousarray(v) for k, v in arrays.items()}


def kernel(**inputs):
    import concourse.bacc as bacc
    from concourse.bass_utils import run_bass_kernel_spmd as run

    arrays = lay_out(**inputs)
    nc = bacc.Bacc("TRN2", target_bir_lowering=False, num_devices=1)
    build(nc, arrays)
    r = run(nc, [{f"in_{n}": a for n, a in arrays.items()}], core_ids=[0])
    return r.results[0]["out_0"].reshape(NB, S, C)[:, 1:]
```

```python
from contextlib import ExitStack, contextmanager

import numpy as np

import concourse.bass as bass
from concourse import mybir

ALU = mybir.AluOpType
ACT = mybir.ActivationFunctionType
AX = mybir.AxisListType
F32 = mybir.dt.float32
F32R = mybir.dt.float32r
F16 = mybir.dt.float16
I32 = mybir.dt.int32

P = 128
NB = 64
GRID = 6
PATCH = 16
NPATCH = GRID * GRID
T = NPATCH + 1
S = T + 1
N = NB * S
NT = N // P
C = 256
KC = C // P
F = 3 * PATCH * PATCH
FK = 7
FP = 116
CH = 8
CW = CH * S
NC = NB // CH
E = 8
NE = E + 1
M = 512
MC = M // P
TOPK = 2
RT = (TOPK * N) // P + E - 1
SH0 = 12
R0 = SH0
R1 = SH0 + RT
HALF = NT // 2
BODY = 8
NF = NT + RT
EARLY = 6
VECTOR_LATE = {2: ("low6", "scale7"), 3: ("largest8",), 4: ("low7",), 5: ("scale8",), 6: ("low8",), 7: ("down6",),
               8: ("down7",), 9: ("down8",)}
SCALAR_LATE = {1: ("high6",), 3: ("high7",), 6: ("high8",), 7: ("down6",), 8: ("down7",), 9: ("down8",)}
SUM_AT = R1 + 3
EPS = 1e-5
NEG = -1e38
XSCALE = 256.0
SCALED = 14
CONSTS = 3 * P + E + NT * E + RT * E + TOPK * NT
XW = 2 * C + 2
POOL_SUMS = 14
PIECES = ((0, 5), (5, 10), (10, 15), (15, NT))
MAGIC = 8388608.0

assert R0 % 2 == 0 and R1 % 2 == 1 and (RT - 5) % BODY == 0 and RT % 4 == 1
assert N % P == 0 and NB % CH == 0 and FK * FP >= F + T + 2 and (NT - 1) % 3 == 0 and (NT - 1) // 3 == EARLY


@contextmanager
def in_steps(engine, first, end, step):
    assert first % step == 0 and end % step == 0
    with engine.Fori(first // step, end // step) as n:
        yield n * step


def wait_apart(engine, sem, value, passed):
    engine.wait_ge(sem, value)
    engine.sem_inc(passed, 1)


class Count:

    def __init__(self, sem):
        self.sem, self.at, self.n = sem, 0, 0

    def up(self, instruction):
        instruction.then_inc(self.sem, 1)
        self.at = self.at + 1
        self.n += 1
        return self.at


def vit_block(nc, x, w_tok, w_attn, chan, w_gate, beta, w_gu, w_down, consts, out):
    ctx = ExitStack()
    with ctx:
        base = (nc.sbuf_base + 31) // 32 * 32
        ctx.enter_context(nc.sbuf_tensor("arena", [P, (nc.sbuf_top - base) // 4 - 16], F32))
        top = base + ((nc.sbuf_top - base) // 4 - 16) * 4
        where = {"at": base}

        def place(name, shape, dt, at=None):
            size = int(np.prod(shape[1:])) * (2 if dt == F16 else 4)
            size = (size + 31) // 32 * 32
            if at is None:
                at = where["at"]
                where["at"] = at + size
                assert where["at"] <= top, name
            return nc.alloc_sbuf_tensor_at(name, shape, dt, offset=at), at + size

        def sem(name):
            return ctx.enter_context(nc.semaphore(name))

        WGU, _ = place("WGU", [P, NE, 2, KC, 2, M], F16)
        WD, _ = place("WD", [P, NE, 2, MC, C], F32R)
        gu_late = base + EARLY * 2 * KC * 2 * M * 2
        d_late = base + NE * 2 * KC * 2 * M * 2 + EARLY * 2 * MC * C * 4
        H, h_end = place("H", [P, NT, C], F32)
        x_at = h_end
        where["at"] = h_end
        XNT, xnt_end = place("XNT", [P, KC, 1 + N], F32)
        where["at"] = xnt_end
        XS, _ = place("XS", [P, NT, XW], F16)
        CH_, _ = place("CHAN", [P, 5, KC], F32)
        WU, _ = place("WU", [P, 3, KC], F32)
        GW, _ = place("GW", [P, KC, E], F32)
        BETA, _ = place("BETA", [P, E], F32)
        AM, _ = place("AM", [P, 2], F32)
        AMALL, _ = place("AMALL", [P, 2], F32)
        SBITS, _ = place("SBITS", [P, 2], I32)
        EXPO, _ = place("EXPO", [P, 2], I32)
        INV, _ = place("INV", [P, NE, 2], I32)
        EPSH, _ = place("EPSH", [P, 2], F32)
        STAT, _ = place("STAT", [P, 3, 6], F32)
        MV, _ = place("MV", [P, 3, 2], F32)
        VE, _ = place("VE", [P, 3, 1], F32)
        RSTD, _ = place("RSTD", [P, 3, 1], F32)
        LG, _ = place("LG", [P, NT, E], F32)
        SG, _ = place("SG", [P, NT, E], F32)
        POS, _ = place("POS", [P, TOPK, NT], I32)
        CW2, _ = place("CW2", [P, TOPK, NT], F32)
        ROW, _ = place("ROW", [P, 4], I32)
        EID, _ = place("EID", [1, NF], I32)
        CONST, _ = place("CONST", [P, CONSTS], F32)
        IDENTH, _ = place("IDENTH", [P, P], F16)

        a = gu_late
        XIN, a = place("XIN", [FP, 3, FK, P], F32, a)
        WTOK, a = place("WTOK", [FP, FK, C], F32, a)
        D, d_end = place("D", [P, 2, KC, CW], F32, a)
        ZERO, a = place("ZERO", [P, XW], F16, d_end)
        assert a <= gu_late + 3 * 8192
        XM, a = place("XM", [P, 2, KC, CW], F32, gu_late)
        KS, a = place("KS", [P, KC, CW], F32, a)
        VS, a = place("VS", [P, 2, KC, CW], F32, a)
        RE, a = place("RE", [P, 2, KC, CW], F32, a)
        assert a <= d_end - 2 * KC * CW * 4
        O, a = place("O", [P, 1 + KC * CW], F32, d_late)
        a = d_late
        XN, a = place("XN", [P, 3, C], F32, a)
        WA, a = place("WA", [P, 4, KC, C], F32, a)
        W38, a = place("W38", [P, KC, CW], F32, a)
        raw_d = a
        RN, a = place("RN", [P, 2, KC, CW], F32, a)
        NUM, a = place("NUM", [P, KC, CW], F32, a)
        Q, a = place("Q", [P, 1 + KC * CW], F32, a)
        assert a <= d_late + 3 * 8192
        RAWD, a = place("RAWD", [P, 2, MC * C], F32, raw_d)
        assert a <= d_late + 3 * 8192
        RAWGU, a = place("RAWGU", [P, 2, 2 * KC * M], F32, xnt_end)
        assert a <= xnt_end + NT * 2 * C * 2
        a = xnt_end
        AE, a = place("AE", [P, 4, KC, CW], F32, a)
        T1, a = place("T1", [P, KC, CW], F32, a)
        DEN, a = place("DEN", [P, KC, CW], F32, a)
        PB, a = place("PB", [P, 1 + KC * CW], F32, a)
        WRM, a = place("WRM", [P, KC, C], F32, (a + 31) // 32 * 32)
        assert a <= xnt_end + NT * 2 * C * 2
        YS, a = place("YS", [P, 3, KC, P], F32, gu_late)
        XT3, a = place("XT3", [P, 3, KC, P], F32, a)
        assert a <= gu_late + 8192

        a = x_at
        XR, a = place("XR", [P, 2, XW], F16, a)
        XT, a = place("XT", [P, 2, 2 * KC, P], F16, a)
        ACTV, a = place("ACTV", [P, 2, M], F32, a)
        HHI, a = place("HHI", [P, 2, MC, P], F32R, a)
        HLO, a = place("HLO", [P, 2, MC, P], F32R, a)
        y_at = a
        Y, y_end = place("Y", [P, 2, C], F32, a)
        assert y_end <= xnt_end
        half = MC * C * 4
        a = d_late + 3 * half
        R8 = [P, NT, E]
        LB, a = place("LB", R8, F32, a)
        EQ, a = place("EQ", R8, F32, a)
        OH, a = place("OH", [P, TOPK, NT, E], F32, a)
        TOT, a = place("TOT", [P, E, NT], F32, a)
        INC, a = place("INC", [P, E, NT], F32, a)
        RED, a = place("RED", [P, NT], F32, a)
        TIL, a = place("TIL", [P, 3, E], F32, a)
        assert a <= d_late + 4 * half
        GE, a = place("GE", [1, RT, E], F32, y_at)
        EIDF, a = place("EIDF", [1, RT], F32, a)
        assert a <= y_end
        ROUTED, a = place("ROUTED", [P, TOPK, NT, C], F32, base + 2 * KC * 2 * M * 2)
        assert a <= base + NE * 2 * KC * 2 * M * 2

        LATE_GU = [place(f"LATE_GU{n}", [P, 2 * KC * M], F32, at)[0]
                   for n, at in enumerate((gu_late + 2 * half, gu_late + 4 * half, d_late))]
        LATE_D = [place(f"LATE_D{n}", [P, MC * C], F32, d_late + at * half)[0] for n, at in enumerate((2, 4, 5))]

        BANK = [ctx.enter_context(nc.psum_tensor(f"bank{n}", [P, 512], F32)) for n in range(8)]
        XTURN = BANK[5][:, 0:C].bitcast(F16)

        xs_slot = nc.dram_tensor("xs_slot", [RT * P, XW], F16, kind="Internal").ap()
        y_routed = nc.dram_tensor("y_routed", [1 + TOPK * N, C], F32, kind="Internal").ap()

        XS_ROW = XS[:, :, 2 * C:XW].bitcast(I32).rearrange("p t a -> p (t a)")
        IDENT = CONST[:, 0:P]
        TRI = CONST[:, P:2 * P]
        ONES = CONST[:, 2 * P:3 * P]
        REV = CONST[:, 3 * P:3 * P + E]
        RESET = CONST[:, 3 * P + E:3 * P + E + NT * E]
        ROWS = CONST[:, CONSTS - TOPK * NT:CONSTS]
        TILES = CONST[0:1, 3 * P + E + NT * E:CONSTS - TOPK * NT].rearrange("p (j e) -> p j e", e=E)
        DECAY, FIRST, MIX = CH_[:, 0, :], CH_[:, 1, :], CH_[:, 2:5, :]
        W_DECAY, W_PLUS_U = WU[:, 0, :], WU[:, 2, :]
        INVF = INV[:, :, :].bitcast(F32)
        SCALE = SBITS[:, :].bitcast(F32)

        def flat(ap):
            return ap.rearrange("p k n -> p (k n)")

        def halves(bank, width):
            return bank[:, 0:2 * width].rearrange("p (k n) -> p k n", k=2)

        w_tok_loaded = sem("w_tok_loaded")
        x_loaded = [sem(f"x_loaded{u}") for u in range(3)]
        consts_loaded = sem("consts_loaded")
        small_loaded = sem("small_loaded")
        raw_loaded = sem("raw_loaded")
        consts_set = sem("consts_set")
        tok_done = sem("tok_done")
        h_ready = sem("h_ready")
        var_ready = sem("var_ready")
        rstd_ready = sem("rstd_ready")
        xn_ready = sem("xn_ready")
        xn_turned = sem("xn_turned")
        xnt_ready = sem("xnt_ready")
        am_ready = sem("am_ready")
        amall_ready = sem("amall_ready")
        scale_ready = sem("scale_ready")
        high_ready = sem("high_ready")
        low_ready = sem("low_ready")
        dlow_ready = sem("dlow_ready")
        act_passed, dve_passed, pool_passed, sp_passed = (
            sem(f"{e}_passed_wait") for e in ("scalar", "vector", "gpsimd", "sync"))
        vstep = sem("vector_step")
        astep = sem("scalar_step")
        decay_ready = sem("decay_ready")
        wrm_ready = sem("wrm_ready")
        diff_ready = sem("diff_ready")
        softplus_ready = sem("softplus_ready")
        mixed = sem("mixed")
        kvr_done = sem("kvr_done")
        kvr_copied = sem("kvr_copied")
        args_ready = sem("args_ready")
        exps_ready = sem("exps_ready")
        relu_ready = sem("relu_ready")
        pb_ready = sem("pb_ready")
        t1_ready = sem("t1_ready")
        bv_ready = sem("bv_ready")
        num_ready = sem("num_ready")
        den_ready = sem("den_ready")
        ln_ready = sem("ln_ready")
        rn_ready = sem("rn_ready")
        s_ready = sem("s_ready")
        e_ready = sem("e_ready")
        y_ready = sem("y_ready")
        zero_stored = sem("zero_stored")
        ys_ready = sem("ys_ready")
        wo_done = sem("wo_done")
        res_ready = sem("res_ready")
        xs_ready = sem("xs_ready")
        xt3_ready = sem("xt3_ready")
        gate_done = sem("gate_done")
        logits_ready = sem("logits_ready")
        ident_ready = sem("ident_ready")
        chosen = sem("chosen")
        prefix_done = sem("prefix_done")
        pos_ready = sem("pos_ready")
        eid_ready = sem("eid_ready")
        coef_ready = sem("coef_ready")
        rows_set = sem("rows_set")
        scattered_first = [sem(f"scattered_first{h}") for h in range(2)]
        scattered_second = sem("scattered_second")
        row_ready = sem("row_ready")
        xr_loaded = [sem(f"xr_loaded{u}") for u in range(2)]
        x_turned = sem("x_turned")
        xt_ready = sem("xt_ready")
        g_done = sem("g_done")
        u_done = sem("u_done")
        silu_ready = sem("silu_ready")
        hid_ready = sem("hid_ready")
        ht_done = sem("ht_done")
        hhi_ready = sem("hhi_ready")
        hlo_ready = sem("hlo_ready")
        down_done = sem("down_done")
        y_copied = sem("y_copied")
        y_stored = [sem(f"y_stored{u}") for u in range(2)]
        late_gu = [sem(f"late_gu{n}") for n in range(NE - EARLY)]
        late_d = [sem(f"late_d{n}") for n in range(NE - EARLY)]
        routed_loaded = [sem(f"routed_loaded{n}") for n in range(len(PIECES))]
        summed = sem("summed")
        pool_summed = sem("pool_summed")
        out_ready = sem("out_ready")
        out_stored = sem("out_stored")

        def late_raw(q):
            return LATE_GU[q - EARLY][:, :], LATE_D[q - EARLY][:, :]

        def by_part(raw_gu):
            r = raw_gu.rearrange("p (g k m) -> p g k m", g=2, k=KC)
            return [r[:, g] for g in range(2)]

        block = ctx.enter_context(nc.Block())

        @block.sync
        def _(sp):
            sp.dma_start(XIN[:, 0], x[0]).then_inc(x_loaded[0], 16)
            for u in range(1, 3):
                sp.dma_start(XIN[:, u], x[u]).then_inc(x_loaded[u], 16)

            def load_raw(q):
                if not isinstance(q, int) or q >= 1:
                    sp.wait_ge(raw_loaded, 32 * q)
                sp.dma_start(RAWGU[:, bass.ds(q % 2, 1), :].rearrange("p a n -> p (a n)"),
                             w_gu[bass.ds(q, 1)].rearrange("a p n -> (a p) n")).then_inc(raw_loaded, 16)
                sp.dma_start(RAWD[:, bass.ds(q % 2, 1), :].rearrange("p a n -> p (a n)"),
                             w_down[bass.ds(q, 1)].rearrange("a p n -> (a p) n")).then_inc(raw_loaded, 16)

            def load_tiles(q):
                for u in range(3):
                    sp.wait_ge(tok_done, 3 * q + u - 2)
                    sp.dma_start(XIN[:, u], x[bass.ds(3 * q + u, 1)].rearrange("a p f n -> (a p) f n"))\
                      .then_inc(x_loaded[u], 16)

            load_raw(0)
            load_tiles(1)
            load_raw(1)
            with sp.Fori(2, EARLY) as q:
                load_tiles(q)
                wait_apart(sp, low_ready, q - 1, sp_passed)
                wait_apart(sp, dlow_ready, q - 1, sp_passed)
                load_raw(q)
            sp.wait_ge(tok_done, NT - 3)
            sp.dma_start(XIN[:, 0], x[NT - 1]).then_inc(x_loaded[0], 16)
            sp.wait_ge(consts_set, 1)
            sp.dma_start(xs_slot.rearrange("(t p) n -> p t n", p=P),
                         ZERO[:, :].rearrange("p (a n) -> p a n", a=1).broadcast_to([P, RT, XW]))\
              .then_inc(zero_stored, 16)
            sp.wait_ge(zero_stored, 16)
            sp.wait_ge(y_ready, NC)
            for n in (0, 1):
                sp.dma_start(late_raw(EARLY + n)[0], w_gu[EARLY + n]).then_inc(late_gu[n], 16)
            sp.dma_start(late_raw(EARLY + 1)[1], w_down[EARLY + 1]).then_inc(late_d[1], 16)
            sp.wait_ge(xs_ready, 2 * NT)
            sp.wait_ge(xn_turned, 2 * NT)
            sp.dma_start(late_raw(NE - 1)[0], w_gu[NE - 1]).then_inc(late_gu[2], 16)
            for n in (0, 2):
                sp.dma_start(late_raw(EARLY + n)[1], w_down[EARLY + n]).then_inc(late_d[n], 16)

            def load_xr(j, u):
                if not isinstance(j, int) or j >= R0 + 2:
                    wait_apart(sp, x_turned, j - 1, sp_passed)
                    wait_apart(sp, row_ready, j - R0 - 1, sp_passed)
                sp.dma_start(XR[:, u], xs_slot[bass.ds((j - R0) * P, P), :]).then_inc(xr_loaded[u], 16)

            sp.wait_ge(scattered_first[0], 16 * HALF)
            sp.wait_ge(scattered_first[1], 16 * (NT - HALF))
            sp.wait_ge(scattered_second, 16 * NT)
            load_xr(R0, 0)
            load_xr(R0 + 1, 1)
            with in_steps(sp, R0 + 2, R1 - 1, 2) as j:
                for u in range(2):
                    load_xr(j + u, u)
            load_xr(R1 - 1, 0)
            for u in range(2):
                sp.wait_ge(y_stored[u], 16 * len(range(R0 + u, R1, 2)))
            for n, (first, end) in enumerate(PIECES):
                for w in range(TOPK):
                    rows = y_routed[1 + w * N + first * P:1 + w * N + end * P]
                    sp.dma_start(ROUTED[:, w, first:end], rows.rearrange("(t p) n -> p t n", p=P))\
                      .then_inc(routed_loaded[n], 16)
            for i in range(NT):
                sp.wait_ge(out_ready, i + 1)
                sp.dma_start(out[i * P:(i + 1) * P, :], H[:, i, :]).then_inc(out_stored, 16)
            sp.wait_ge(out_stored, 16 * NT)

        @block.tensor
        def _(pe):
            def tok(i, u):
                pe.wait_ge(x_loaded[u], 16 * (i // 3 + 1))
                for f in range(FK):
                    last = nc.tensor.matmul(BANK[u][:, 0:C], XIN[:, u, f, :], WTOK[:, f, :],
                                            start=f == 0, stop=f == FK - 1)
                last.then_inc(tok_done, 1)

            def turn(i, u, count):
                pe.wait_ge(xn_ready, count + 1)
                for k in range(KC):
                    last = nc.tensor.transpose(BANK[3 + u][:, k * P:(k + 1) * P], XN[:, u, k * P:(k + 1) * P], IDENT)
                last.then_inc(xn_turned, 1)

            pe.wait_ge(w_tok_loaded, 16)
            def product(banks, pairs):
                for m in range(KC):
                    for k, (w, x) in enumerate(pairs):
                        last = nc.tensor.matmul(BANK[banks + m][:, 0:CW], w[:, m * P:(m + 1) * P], x,
                                                start=k == 0, stop=k == len(pairs) - 1)
                last.then_inc(kvr_done, 1)

            def receptance(c):
                if isinstance(c, int):
                    pe.wait_ge(small_loaded, 16 * 3)
                    pe.wait_ge(wrm_ready, 1)
                else:
                    pe.wait_ge(kvr_copied, 3 * c - 2)
                pe.wait_ge(diff_ready, c + 1)
                d = D[:, bass.ds(c % 2, 1)].rearrange("p a k n -> p (a k) n")
                product(6, [(WA[:, 2, k], XNT[:, k, bass.ds(c * CW, CW)]) for k in range(KC)]
                        + [(WRM[:, k], d[:, k]) for k in range(KC)])

            def key_value(c):
                for o in range(2):
                    if isinstance(c, int):
                        pe.wait_ge(xnt_ready, NT)
                    else:
                        pe.wait_ge(kvr_copied, 3 * c)
                    pe.wait_ge(mixed, 2 * c + o + 1)
                    product(2 * o, [(WA[:, o, k], XM[:, o, k, :]) for k in range(KC)])

            tok(0, 0)
            tok(1, 1)
            pe.wait_ge(consts_loaded, 16 * 4)
            with in_steps(pe, 0, NT - 4, 3) as b:
                for u in range(3):
                    tok(b + (u + 2), (u + 2) % 3)
                    turn(b + u, u, b + u)
            for i in range(NT - 4, NT):
                if i + 2 < NT:
                    tok(i + 2, (i + 2) % 3)
                if i == NT - 2:
                    receptance(0)
                turn(i, i % 3, i)

            key_value(0)
            with pe.Fori(1, NC) as c:
                receptance(c)
                key_value(c)

            def wo(i, u):
                pe.wait_ge(ys_ready, i + 1)
                for k in range(KC):
                    last = nc.tensor.matmul(BANK[u][:, 0:C], YS[:, u, k, :], WA[:, 3, k, :], start=k == 0, stop=k == KC - 1)
                last.then_inc(wo_done, 1)

            def gate(i, u):
                pe.wait_ge(xt3_ready, i + 1)
                if not isinstance(i, int) or i >= 1:
                    pe.wait_ge(logits_ready, i)
                for k in range(KC):
                    last = nc.tensor.matmul(BANK[6][:, 0:E], XT3[:, u, k, :], GW[:, k, :], start=k == 0, stop=k == KC - 1)
                last.then_inc(gate_done, 1)

            pe.wait_ge(kvr_copied, 3 * NC)
            wo(0, 0)
            wo(1, 1)

            def token_tiles(b, end=3):
                for u in range(end):
                    i = b + u
                    if not isinstance(i, int) or i + 2 < NT:
                        wo(i + 2, (u + 2) % 3)
                    turn(i, u, i + NT)
                    if not isinstance(i, int) or i >= 1:
                        gate(i - 1, (u + 2) % 3)

            token_tiles(0)
            with in_steps(pe, 3, NT - 4, 3) as b:
                token_tiles(b)
            token_tiles(NT - 4)
            token_tiles(NT - 1, 1)
            gate(NT - 1, (NT - 1) % 3)

            def turn_x(j, u, shared):
                if shared:
                    pe.wait_ge(xs_ready, 2 * NT)
                    x = XS[:, bass.ds(j if not isinstance(j, int) or j < R0 else j - RT, 1), :]\
                        .rearrange("p a n -> p (a n)")
                else:
                    pe.wait_ge(xr_loaded[u], 8 * (j - R0 - u) + 16)
                    x = XR[:, u]
                if not isinstance(j, int) or j >= 1:
                    pe.wait_ge(xt_ready, j)
                for k in range(2 * KC):
                    last = nc.tensor.transpose(XTURN[:, k * P:(k + 1) * P], x[:, k * P:(k + 1) * P], IDENTH[:, :])
                last.then_inc(x_turned, 1)

            def gate_up(j, u, e):
                pe.wait_ge(xt_ready, j + 1)
                for g, done in ((0, g_done), (1, u_done)):
                    if not isinstance(j, int) or j >= 2:
                        pe.wait_ge((silu_ready, hid_ready)[g], j - 1)
                    n = 0
                    for k in range(KC):
                        for xh, wh in ((0, 0), (0, 1), (1, 0)):
                            w = WGU[:, bass.ds(e, 1), g, k, wh, :].rearrange("p a n -> p (a n)")
                            last = nc.tensor.matmul(BANK[2 * g + u][:, :], XT[:, u, xh * KC + k, :], w,
                                                    start=n == 0, stop=n == 3 * KC - 1)
                            n += 1
                    last.then_inc(done, 1)

            def turn_hidden(j, u):
                pe.wait_ge(hid_ready, j + 1)
                if not isinstance(j, int) or j >= 1:
                    pe.wait_ge(hlo_ready, j)
                for m in range(MC):
                    last = nc.tensor.transpose(BANK[4][:, m * P:(m + 1) * P], ACTV[:, u, m * P:(m + 1) * P], IDENT)
                last.then_inc(ht_done, 1)

            def down(j, u, e):
                pe.wait_ge(hlo_ready, j + 1)
                if not isinstance(j, int) or j >= 2:
                    pe.wait_ge(y_copied, j - 1)
                n = 0
                for m in range(MC):
                    for hid, wh in ((HHI, 0), (HHI, 1), (HLO, 0)):
                        w = WD[:, bass.ds(e, 1), wh, m, :].rearrange("p a n -> p (a n)")
                        last = nc.tensor.matmul(BANK[6 + u][:, 0:C], hid[:, u, m, :], w,
                                                start=n == 0, stop=n == 3 * MC - 1)
                        n += 1
                last.then_inc(down_done, 1)

            pe.wait_ge(logits_ready, NT)
            pe.wait_ge(ident_ready, 1)
            pe.wait_ge(low_ready, 1)
            pe.wait_ge(dlow_ready, 1)
            def feed(j, u, e, e2, turn_next):
                gate_up(j, u, e)
                if turn_next is not None:
                    turn_x(j + 1, 1 - u, turn_next)
                turn_hidden(j - 1, 1 - u)
                down(j - 2, u, e2)

            def chosen_expert(j):
                return pe.value_load(EID[0:1, bass.ds(j, 1)], min_val=0, max_val=NE - 1)

            SHARED, ROUTED_NEXT = True, False
            turn_x(0, 0, True)
            turn_x(1, 1, True)
            gate_up(0, 0, 0)
            turn_x(2, 0, True)
            pe.wait_ge(chosen, 1)
            nc.tensor.matmul(BANK[7][:, 0:NT * E], TRI, LB[:, :, :].rearrange("p t e -> p (t e)"), start=True, stop=True)
            nc.tensor.matmul(BANK[7][:, 256:256 + NT * E], ONES, LB[:, :, :].rearrange("p t e -> p (t e)"),
                             start=True, stop=True).then_inc(prefix_done, 1)
            gate_up(1, 1, 0)
            turn_hidden(0, 0)
            gate_up(2, 0, 0)
            turn_x(3, 1, True)
            turn_hidden(1, 1)
            down(0, 0, 0)
            turn_x(4, 0, True)
            gate_up(3, 1, 0)
            turn_hidden(2, 0)
            pe.wait_ge(pos_ready, 1)
            down(1, 1, 0)
            with in_steps(pe, 4, R0 - 2, 2) as j:
                for u in range(2):
                    feed(j + u, u, 0, 0, SHARED)
            feed(R0 - 2, 0, 0, 0, SHARED)
            feed(R0 - 1, 1, 0, 0, None)
            turn_x(R0, 0, False)
            pe.wait_ge(eid_ready, 1)
            pe.wait_ge(low_ready, NE)
            feed(R0, 0, chosen_expert(R0), 0, ROUTED_NEXT)
            feed(R0 + 1, 1, chosen_expert(R0 + 1), 0, ROUTED_NEXT)
            pe.wait_ge(dlow_ready, NE)
            for j in (R0 + 2, R0 + 3):
                feed(j, j % 2, chosen_expert(j), chosen_expert(j - 2), ROUTED_NEXT)
            with pe.Fori(0, (R1 - 1 - (R0 + 4)) // BODY) as n:
                j = n * BODY + (R0 + 4)
                for u in range(BODY):
                    feed(j + u, u % 2, chosen_expert(j + u), chosen_expert(j + (u - 2)), ROUTED_NEXT)
            for j in (R1 - 1, R1, R1 + 1, R1 + 2):
                feed(j, j % 2, chosen_expert(j) if j < R1 else 0, chosen_expert(j - 2) if j < R1 + 2 else 0, SHARED)
            for j in range(R1 + 3, NF - 1):
                feed(j, j % 2, 0, 0, SHARED)
            feed(NF - 1, 1, 0, 0, None)
            turn_hidden(NF - 1, 1)
            down(NF - 2, 0, 0)
            down(NF - 1, 1, 0)

        @block.scalar
        def _(act):
            act.dma_start(WTOK[:, :, :], w_tok).then_inc(w_tok_loaded, 16)
            for dst, src in ((CONST, consts), (CH_, chan), (GW, w_gate), (BETA, beta)):
                act.dma_start(dst[tuple(slice(None) for _ in dst.shape)], src).then_inc(consts_loaded, 16)
            for o in range(0, 3):
                n = (0, 2, 3, 4)
                act.dma_start(WA[:, n[o]:n[o + 1]], w_attn[:, n[o]:n[o + 1]]).then_inc(small_loaded, 16)
            step = Count(astep)

            act.wait_ge(consts_loaded, 16 * 4)
            nc.scalar.activation(WU[:, 1, :], DECAY, ACT.Exp).then_inc(decay_ready, 1)

            def copy_h(i, u):
                act.wait_ge(tok_done, i + 1)
                nc.scalar.activation(H[:, bass.ds(i, 1), :].rearrange("p a n -> p (a n)"), BANK[u][:, 0:C], ACT.Copy)\
                  .then_inc(h_ready, 1)

            def copy_xnt(i, u):
                act.wait_ge(xn_turned, i + 1)
                nc.scalar.activation(XNT[:, :, bass.ds(i * P + 1, P)], halves(BANK[3 + u], P), ACT.Copy)\
                  .then_inc(xnt_ready, 1)

            def high_gu(q, gu):
                act.wait_ge(scale_ready, q + 1)
                for g in range(2):
                    nc.scalar.activation(WGU[:, bass.ds(q, 1), g, :, 0, :].rearrange("p a k m -> p (a k) m"),
                                         gu[g], ACT.Copy, scale=SCALE[:, g:g + 1]).then_inc(high_ready, 1)

            def high_d(q, raw):
                nc.scalar.activation(WD[:, bass.ds(q, 1), 0].rearrange("p a m n -> p (a m n)"), raw, ACT.Copy)\
                  .then_inc(high_ready, 1)

            def raw_gu(q):
                r = RAWGU[:, bass.ds(q % 2, 1), :].rearrange("p a (g k m) -> p (a g) k m", g=2, k=KC)
                return [r[:, g] for g in range(2)]

            def first_tiles(b):
                q = b // 3
                for u in range(3):
                    if not isinstance(b, int) or b + u + 2 < NT:
                        copy_h(b + (u + 2), (u + 2) % 3)
                    copy_xnt(b + u, u)
                    if u == 0:
                        wait_apart(act, raw_loaded, 32 * q + 32, act_passed)
                        high_d(q, RAWD[:, bass.ds(q % 2, 1), :].rearrange("p a n -> p (a n)"))
                    if u == 1:
                        high_gu(q, raw_gu(q))

            copy_h(0, 0)
            copy_h(1, 1)
            with in_steps(act, 0, NT - 4, 3) as b:
                first_tiles(b)
            first_tiles(NT - 4)
            copy_xnt(NT - 1, (NT - 1) % 3)

            def copy_kvr(c):
                s = c % 2
                act.wait_ge(kvr_done, 3 * c + 1)
                for m in range(KC):
                    nc.scalar.activation(RN[:, bass.ds(s, 1), m, :].rearrange("p a n -> p (a n)"),
                                         BANK[6 + m][:, 0:CW], ACT.Relu, scale=-1.0)
                for m in range(KC):
                    i = nc.scalar.activation(RE[:, bass.ds(s, 1), m, :].rearrange("p a n -> p (a n)"),
                                             BANK[6 + m][:, 0:CW], ACT.Abs)
                i.then_inc(kvr_copied, 1)
                act.wait_ge(kvr_done, 3 * c + 2)
                if not isinstance(c, int) or c >= 1:
                    act.wait_ge(args_ready, 2 * c)
                for m in range(KC):
                    i = nc.scalar.activation(KS[:, m, :], BANK[m][:, 0:CW], ACT.Copy)
                i.then_inc(kvr_copied, 1)
                act.wait_ge(kvr_done, 3 * c + 3)
                for m in range(KC):
                    i = nc.scalar.activation(VS[:, bass.ds(s, 1), m, :].rearrange("p a n -> p (a n)"),
                                             BANK[2 + m][:, 0:CW], ACT.Copy)
                i.then_inc(kvr_copied, 1)
                wait_apart(act, kvr_copied, 3 * c + 1, act_passed)
                re = RE[:, bass.ds(s, 1)].rearrange("p a k n -> p (a k n)")
                step.up(nc.scalar.activation(re, re, ACT.Exp, scale=-1.0))
                wait_apart(act, astep, c + 1, act_passed)
                nc.scalar.activation(re, re, ACT.Ln, bias=1.0).then_inc(softplus_ready, 1)

            def exps(c, last):
                for n, scale in enumerate((1.0, -1.0)):
                    act.wait_ge(args_ready, 2 * c + n + 1)
                    nc.scalar.activation(flat(AE[:, n]), flat(AE[:, n]), ACT.Exp, scale=scale).then_inc(exps_ready, 1)
                if last is not None:
                    ratio(last)
                nc.scalar.activation(flat(AE[:, 2]), flat(AE[:, 3]), ACT.Relu).then_inc(relu_ready, 1)
                act.wait_ge(relu_ready, 2 * c + 1)
                nc.scalar.activation(flat(AE[:, 3]), flat(AE[:, 3]), ACT.Relu, scale=-1.0).then_inc(relu_ready, 1)
                act.wait_ge(relu_ready, 2 * c + 2)
                ae = AE[:, 2:4].rearrange("p n k m -> p (n k m)")
                nc.scalar.activation(ae, ae, ACT.Exp, scale=-1.0).then_inc(exps_ready, 1)

            def logarithm(c):
                act.wait_ge(den_ready, c + 1)
                nc.scalar.activation(flat(DEN[:, :, :]), flat(DEN[:, :, :]), ACT.Ln).then_inc(ln_ready, 1)

            def ratio(c):
                act.wait_ge(s_ready, c + 1)
                nc.scalar.activation(flat(DEN[:, :, :]), flat(DEN[:, :, :]), ACT.Exp, scale=-1.0).then_inc(e_ready, 1)

            def copy_ys(i, u, chunks=NC):
                act.wait_ge(y_ready, chunks)
                nc.scalar.activation(YS[:, u], XNT[:, :, bass.ds(i * P + 1, P)], ACT.Copy).then_inc(ys_ready, 1)

            nc.scalar.preload_act_table_set("natural_log_exp_and_others")
            act.wait_ge(dlow_ready, EARLY)
            copy_kvr(0)
            exps(0, None)
            copy_kvr(1)
            with act.Fori(1, NC - 1) as c:
                logarithm(c - 1)
                exps(c, c - 1)
                copy_kvr(c + 1)
            logarithm(NC - 2)
            for i in range(3):
                copy_ys(i, i, 2)
            exps(NC - 1, NC - 2)
            logarithm(NC - 1)
            ratio(NC - 1)

            def copy_xt3(i, u):
                act.wait_ge(xn_turned, i + (NT + 1))
                nc.scalar.activation(XT3[:, u], halves(BANK[3 + u], P), ACT.Copy).then_inc(xt3_ready, 1)

            def copy_logits(i):
                act.wait_ge(gate_done, i + 1)
                nc.scalar.activation(LG[:, bass.ds(i, 1), :].rearrange("p a n -> p (a n)"), BANK[6][:, 0:E], ACT.Copy)\
                  .then_inc(logits_ready, 1)

            def token_tiles(b, end=3, chunks=NC):
                for u in range(end):
                    i = b + u
                    if not isinstance(i, int) or i + 3 < NT:
                        act.wait_ge(wo_done, i + 1)
                        copy_ys(i + 3, u, chunks)
                    copy_xt3(i, u)
                    if not isinstance(i, int) or i >= 1:
                        copy_logits(i - 1)

            token_tiles(0, chunks=NC - 1)
            with in_steps(act, 3, NT - 4, 3) as b:
                token_tiles(b)
            token_tiles(NT - 4)
            token_tiles(NT - 1, 1)
            copy_logits(NT - 1)

            def silu(j, u, e):
                act.wait_ge(g_done, j + 1)
                if not isinstance(j, int) or j >= 2:
                    act.wait_ge(ht_done, j - 1)
                nc.scalar.activation(ACTV[:, u], BANK[u][:, :], ACT.Silu,
                                     scale=INVF[:, bass.ds(e, 1), 0]).then_inc(silu_ready, 1)

            def hidden_high(j, u):
                act.wait_ge(ht_done, j + 1)
                if not isinstance(j, int) or j >= 2:
                    act.wait_ge(down_done, j - 1)
                nc.scalar.activation(HHI[:, u].rearrange("p m n -> p (m n)"), BANK[4][:, :], ACT.Copy)\
                  .then_inc(hhi_ready, 1)

            def feed(j, u, e):
                silu(j, u, e)
                hidden_high(j - 1, 1 - u)

            def chosen_expert(j):
                return act.value_load(EID[0:1, bass.ds(j, 1)], min_val=0, max_val=NE - 1)

            act.wait_ge(logits_ready, NT)
            nc.scalar.activation(SG[:, :, :], LG[:, :, :], ACT.Sigmoid).then_inc(coef_ready, 1)
            silu(0, 0, 0)
            for j in range(1, R0):
                feed(j, j % 2, 0)
                for late in SCALAR_LATE.get(j, ()):
                    what, q = late[:-1], int(late[-1])
                    if what == "high":
                        high_gu(q, by_part(late_raw(q)[0]))
                    else:
                        act.wait_ge(late_d[q - EARLY], 16)
                        if q == EARLY:
                            act.wait_ge(low_ready, NE)
                        else:
                            act.wait_ge(dlow_ready, q)
                        high_d(q, late_raw(q)[1])
            act.wait_ge(eid_ready, 1)
            with in_steps(act, R0, R1 + 1, 2) as j:
                for u in range(2):
                    feed(j + u, u, chosen_expert(j + u))
            with in_steps(act, R1 + 1, NF, 2) as j:
                for u in range(2):
                    feed(j + u, u, 0)
            hidden_high(NF - 1, 1)

        @block.vector
        def _(dve):
            step = Count(vstep)

            def then(mark):
                dve.wait_ge(vstep, mark)

            def after(instruction):
                then(step.up(instruction))

            step.up(nc.vector.memset(XNT[:, :, 0:1], 0.0))
            step.up(nc.vector.memset(W38[:, :, :], 0.0))
            step.up(nc.vector.memset(EID[:, :], 0))
            nc.vector.memset(EPSH[:, 1:2], -0.5).then_inc(var_ready, 1)
            dve.wait_ge(decay_ready, 1)
            after(nc.vector.tensor_scalar(W_DECAY, WU[:, 1, :], -1.0, None, ALU.mult))
            step.up(nc.vector.tensor_tensor(W_PLUS_U, FIRST, W_DECAY, ALU.add))
            for k in range(KC):
                after(nc.vector.tensor_scalar(W38[:, k, :], W38[:, k, :], W_DECAY[:, k:k + 1], None, ALU.add))
            after(nc.vector.memset(W38[:, :, :].rearrange("p k (b s) -> p k b s", s=S)[:, :, :, 0], 2 * NEG))

            def tile_of(i):
                return H[:, bass.ds(i, 1), :].rearrange("p a n -> p (a n)")

            def stats(i, u):
                return step.up(nc.vector.bn_stats(STAT[:, u], tile_of(i)))

            def variance(u, mark):
                wait_apart(dve, vstep, mark, dve_passed)
                return step.up(nc.vector.bn_aggr(MV[:, u], STAT[:, u]))

            def var_eps(u, mark):
                then(mark)
                nc.vector.tensor_scalar(VE[:, u], MV[:, u, 1:2], EPS, None, ALU.add).then_inc(var_ready, 1)

            def affine(i, u, count):
                dve.wait_ge(rstd_ready, count + 1)
                nc.vector.tensor_scalar(XN[:, u], tile_of(i), MV[:, u, 0:1], RSTD[:, u], ALU.subtract, ALU.mult)\
                  .then_inc(xn_ready, 1)

            def largest(q, gu):
                nc.vector.tensor_reduce(AM[:, :], gu, AX.X, ALU.max,
                                        apply_absolute_value=True).then_inc(am_ready, 1)

            def scales(q):
                dve.wait_ge(amall_ready, q + 1)
                after(nc.vector.tensor_scalar(EXPO[:, :], AMALL[:, :].bitcast(I32), 0x7F800000, None, ALU.bitwise_and))
                inv = INV[:, bass.ds(q, 1), :].rearrange("p a n -> p (a n)")
                after(nc.vector.tensor_scalar(inv, EXPO[:, :], float(30 << 23), float((SCALED + 8) << 23),
                                              ALU.max, ALU.subtract))
                nc.vector.tensor_scalar(SBITS[:, :], inv, -1.0, float(246 << 23), ALU.mult, ALU.add)\
                  .then_inc(scale_ready, 1)

            def split_low(q, gu, high):
                dve.wait_ge(scale_ready, q + 1)
                for g in range(2):
                    dve.wait_ge(high_ready, high + (g + 1))
                    w = WGU[:, bass.ds(q, 1), g].rearrange("p a k h m -> p (a k) h m")
                    last = nc.vector.scalar_tensor_tensor(w[:, :, 1], gu[g], SCALE[:, g:g + 1], w[:, :, 0],
                                                          ALU.mult, ALU.subtract)
                last.then_inc(low_ready, 1)

            def raw_gu(q):
                r = RAWGU[:, bass.ds(q % 2, 1), :].rearrange("p a (g k m) -> p (a g) k m", g=2, k=KC)
                return [r[:, g] for g in range(2)]

            dve.wait_ge(h_ready, 1)
            var_eps(0, variance(0, stats(0, 0)))
            nc.vector.tensor_copy(IDENTH[:, :], IDENT).then_inc(ident_ready, 1)
            dve.wait_ge(small_loaded, 16 * 3)
            for k in range(KC):
                i = nc.vector.tensor_scalar(WRM[:, k], WA[:, 2, k], MIX[:, 2, k:k + 1], None, ALU.mult)
            i.then_inc(wrm_ready, 1)
            start = step.at
            with in_steps(dve, 0, NT - 1, 3) as b:
                q = b // 3
                step.at = start + q * 8
                n0 = step.n
                for u in range(3):
                    n = (u + 1) % 3
                    dve.wait_ge(h_ready, b + (u + 2))
                    mark = stats(b + (u + 1), n)
                    affine(b + u, u, b + u)
                    var_eps(n, variance(n, mark))
                    if u == 0:
                        wait_apart(dve, raw_loaded, 32 * q + 32, dve_passed)
                        largest(q, RAWGU[:, bass.ds(q % 2, 1), :].rearrange("p a (g n) -> p (a g) n", g=2))
                    if u == 1:
                        scales(q)
                    if u == 2:
                        split_low(q, raw_gu(q), 3 * q + 1)
                assert step.n - n0 == 8
            step.at = start + EARLY * 8
            affine(NT - 1, 0, NT - 1)

            def mix(c):
                dve.wait_ge(diff_ready, c + 1)
                xx = XNT[:, :, bass.ds(c * CW, CW)]
                d = D[:, bass.ds(c % 2, 1)].rearrange("p a k n -> p (a k) n")
                for o in range(2):
                    if not isinstance(c, int) or c >= 1:
                        dve.wait_ge(kvr_done, 3 * c - 1 + o)
                    for k in range(KC):
                        i = nc.vector.scalar_tensor_tensor(XM[:, o, k, :], d[:, k, :], MIX[:, o, k:k + 1], xx[:, k, :],
                                                           ALU.mult, ALU.add)
                    i.then_inc(mixed, 1)

            def scan_max(c):
                dve.wait_ge(kvr_copied, 3 * c + 2)
                after(nc.vector.memset(KS[:, :, :].rearrange("p k (b s) -> p k b s", s=S)[:, :, :, 0], NEG))
                after(nc.vector.tensor_tensor_scan(O[:, 1:], flat(W38[:, :, :]), flat(KS[:, :, :]), NEG, ALU.add, ALU.max))
                if not isinstance(c, int) or c >= 1:
                    dve.wait_ge(t1_ready, c)
                for k in range(KC):
                    i = nc.vector.scalar_tensor_tensor(AE[:, 3, k, :], O[:, k * CW:(k + 1) * CW], FIRST[:, k:k + 1],
                                                       KS[:, k, :], ALU.subtract, ALU.subtract)
                    step.up(i)
                then(step.at)
                for n, op in ((0, ALU.min), (1, ALU.max)):
                    for k in range(KC):
                        i = nc.vector.tensor_scalar(AE[:, n, k, :], AE[:, 3, k, :], W_PLUS_U[:, k:k + 1], 0.0, ALU.add, op)
                    i.then_inc(args_ready, 1)

            def scan_sums(c):
                dve.wait_ge(exps_ready, 3 * c + 2)
                a2, b2, bb, aa = (flat(AE[:, n]) for n in range(4))
                step.up(nc.vector.tensor_tensor_scan(Q[:, 1:], a2, b2, 0.0, ALU.mult, ALU.add))
                q_mark = step.at
                dve.wait_ge(kvr_copied, 3 * c + 3)
                vs = VS[:, bass.ds(c % 2, 1)].rearrange("p a k n -> p (a k n)")
                then(q_mark)
                after(nc.vector.tensor_tensor(b2, b2, vs, ALU.mult))
                nc.vector.tensor_tensor_scan(PB[:, 1:], a2, b2, 0.0, ALU.mult, ALU.add).then_inc(pb_ready, 1)
                dve.wait_ge(exps_ready, 3 * c + 3)
                after(nc.vector.tensor_tensor(flat(DEN[:, :, :]), aa, Q[:, 0:KC * CW], ALU.mult))
                nc.vector.tensor_tensor(flat(DEN[:, :, :]), flat(DEN[:, :, :]), bb, ALU.add).then_inc(den_ready, 1)

            def finish(c):
                dve.wait_ge(e_ready, c + 1)
                dve.wait_ge(num_ready, c + 1)
                nc.vector.tensor_tensor(XNT[:, :, bass.ds(c * CW + 1, CW)], NUM[:, :, :], DEN[:, :, :], ALU.mult)\
                  .then_inc(y_ready, 1)

            PER = 7
            dve.wait_ge(tok_done, NT)
            mix(0)
            dve.wait_ge(low_ready, EARLY)
            dve.wait_ge(dlow_ready, EARLY)
            dve.wait_ge(xn_turned, NT)
            step.up(nc.vector.memset(O[:, 0:1], NEG))
            step.up(nc.vector.memset(PB[:, 0:1], 0.0))
            after(nc.vector.memset(Q[:, 0:1], 0.0))
            start = step.at
            n0 = step.n
            scan_max(0)
            mix(1)
            scan_sums(0)
            assert step.n - n0 == PER, step.n - n0
            with dve.Fori(1, NC - 1) as c:
                step.at = start + PER * c
                scan_max(c)
                mix(c + 1)
                finish(c - 1)
                scan_sums(c)
            step.at = start + PER * (NC - 1)
            scan_max(NC - 1)
            finish(NC - 2)

            def residual(i, u):
                dve.wait_ge(wo_done, i + 1)
                nc.vector.tensor_tensor(tile_of(i), BANK[u][:, 0:C], tile_of(i), ALU.add).then_inc(res_ready, 1)

            def out_stats(i, u):
                wait_apart(dve, res_ready, i + 1, dve_passed)
                return stats(i, u)

            def parts(i, u, part):
                xs = XS[:, bass.ds(i, 1), 0:2 * C].rearrange("p a (h n) -> p (a h) n", h=2)
                if part == 0:
                    dve.wait_ge(xn_ready, i + NT + 1)
                    nc.vector.tensor_scalar(xs[:, 0], XN[:, u], XSCALE, None, ALU.mult).then_inc(xs_ready, 1)
                else:
                    dve.wait_ge(xs_ready, 2 * i + 1)
                    nc.vector.scalar_tensor_tensor(xs[:, 1], XN[:, u], XSCALE, xs[:, 0], ALU.mult, ALU.subtract)\
                      .then_inc(xs_ready, 1)

            def token_step(i, u):
                n = (u + 1) % 3
                residual(i + 1, n)
                if not isinstance(i, int) or i >= 1:
                    parts(i - 1, (u + 2) % 3, 1)
                mark = out_stats(i + 1, n)
                affine(i, u, i + NT)
                mark = variance(n, mark)
                parts(i, u, 0)
                var_eps(n, mark)

            residual(0, 0)
            var_eps(0, variance(0, out_stats(0, 0)))
            scan_sums(NC - 1)
            start = step.at
            token_step(0, 0)
            token_step(1, 1)
            finish(NC - 1)
            dve.wait_ge(y_ready, NC)
            nc.vector.tensor_copy(XS_ROW, ROWS[:, 0:NT]).then_inc(rows_set, 1)
            token_step(2, 2)
            with in_steps(dve, 3, NT - 1, 3) as b:
                step.at = start + b * 2
                for u in range(3):
                    token_step(b + u, u)
            step.at = start + 2 * (NT - 1)
            parts(NT - 2, (NT - 2) % 3, 1)
            affine(NT - 1, 0, 2 * NT - 1)
            parts(NT - 1, 0, 0)
            parts(NT - 1, 0, 1)

            def copy_xt(j, u):
                dve.wait_ge(x_turned, j + 1)
                if not isinstance(j, int) or j >= 2:
                    dve.wait_ge(u_done, j - 1)
                nc.vector.tensor_copy(XT[:, u].rearrange("p k n -> p (k n)"), XTURN).then_inc(xt_ready, 1)

            def hidden(j, u, e):
                dve.wait_ge(silu_ready, j + 1)
                dve.wait_ge(u_done, j + 1)
                nc.vector.scalar_tensor_tensor(ACTV[:, u], BANK[2 + u][:, :], INVF[:, bass.ds(e, 1), 1], ACTV[:, u],
                                               ALU.mult, ALU.mult).then_inc(hid_ready, 1)

            def hidden_low(j, u):
                dve.wait_ge(hhi_ready, j + 1)
                nc.vector.tensor_tensor(HLO[:, u].rearrange("p m n -> p (m n)"), BANK[4][:, :],
                                        HHI[:, u].rearrange("p m n -> p (m n)"), ALU.subtract).then_inc(hlo_ready, 1)

            def late_largest(q):
                dve.wait_ge(late_gu[q - EARLY], 16)
                largest(q, late_raw(q)[0].rearrange("p (g n) -> p g n", g=2))

            late_largest(EARLY)
            copy_xt(0, 0)
            copy_xt(1, 1)
            dve.wait_ge(logits_ready, NT)
            rev = REV.rearrange("p (a e) -> p a e", a=1).broadcast_to(R8)

            def over_e(ap):
                return ap.rearrange("p (t a) -> p t a", a=1).broadcast_to(R8)

            after(nc.vector.tensor_tensor(LB[:, :, :], LG[:, :, :],
                                          BETA[:, :].rearrange("p (a e) -> p a e", a=1).broadcast_to(R8), ALU.add))
            for w in range(TOPK):
                after(nc.vector.tensor_reduce(RED[:, :], LB[:, :, :], AX.X, ALU.max))
                after(nc.vector.tensor_tensor(EQ[:, :, :], LB[:, :, :], over_e(RED[:, :]), ALU.is_equal))
                after(nc.vector.tensor_tensor(EQ[:, :, :], EQ[:, :, :], rev, ALU.mult))
                after(nc.vector.tensor_reduce(RED[:, :], EQ[:, :, :], AX.X, ALU.max))
                after(nc.vector.tensor_tensor(OH[:, w], EQ[:, :, :], over_e(RED[:, :]), ALU.is_equal))
                if w == 0:
                    after(nc.vector.scalar_tensor_tensor(LB[:, :, :], OH[:, 0], NEG, LB[:, :, :], ALU.mult, ALU.add))
            nc.vector.tensor_tensor(LB[:, :, :], OH[:, 0], OH[:, 1], ALU.add).then_inc(chosen, 1)
            def late_down_low(q):
                dve.wait_ge(high_ready, 2 * NE + q + 1)
                nc.vector.tensor_tensor(WD[:, q, 1].rearrange("p m n -> p (m n)"), late_raw(q)[1],
                                        WD[:, q, 0].rearrange("p m n -> p (m n)").bitcast(F32), ALU.subtract)\
                  .then_inc(dlow_ready, 1)

            def add_y(j, u):
                dve.wait_ge(down_done, j + 1)
                i = j if j < R0 else j - RT
                nc.vector.tensor_tensor(H[:, i], BANK[6 + u][:, 0:C], H[:, i], ALU.add).then_inc(y_copied, 1)

            def copy_y(j, u):
                dve.wait_ge(down_done, j + 1)
                if not isinstance(j, int) or j >= R0 + 2:
                    dve.wait_ge(y_stored[u], 8 * (j - R0 - u))
                nc.vector.tensor_copy(Y[:, u], BANK[6 + u][:, 0:C]).then_inc(y_copied, 1)

            def feed(j, u, e, out_y, copy_next=True):
                hidden(j, u, e)
                if copy_next:
                    copy_xt(j + 1, 1 - u)
                hidden_low(j - 1, 1 - u)
                out_y(j - 2, u)

            copy_xt(2, 0)
            hidden(0, 0, 0)
            dve.wait_ge(prefix_done, 1)
            dve.wait_ge(chosen, 1)
            after(nc.vector.tensor_copy(TOT[:, :, :], BANK[7][:, 256:256 + NT * E].rearrange("p (t e) -> p e t", e=E)))
            after(nc.vector.tensor_tensor_scan(INC[:, :, :].rearrange("p e t -> p (e t)"), RESET,
                                               TOT[:, :, :].rearrange("p e t -> p (e t)"), 0.0, ALU.mult, ALU.add))
            after(nc.vector.tensor_scalar(TIL[:, 0], INC[:, :, NT - 1], 1.0 / P, 0.5 - 0.25 / P, ALU.mult, ALU.add))
            step.up(nc.vector.tensor_tensor(INC[:, :, :], INC[:, :, :], TOT[:, :, :], ALU.subtract))
            after(nc.vector.tensor_scalar(TIL[:, 0], TIL[:, 0], MAGIC, MAGIC, ALU.add, ALU.subtract))
            after(nc.vector.tensor_tensor_scan(TIL[:, 1], ONES[:, 0:E], TIL[:, 0], 0.0, ALU.mult, ALU.add))
            after(nc.vector.tensor_tensor(TIL[:, 2], TIL[:, 1], TIL[:, 0], ALU.subtract))
            after(nc.vector.tensor_scalar(TIL[:, 2], TIL[:, 2], float(P), None, ALU.mult))
            after(nc.vector.tensor_tensor(INC[:, :, :], INC[:, :, :],
                                          TIL[:, 2].rearrange("p (e a) -> p e a", a=1).broadcast_to([P, E, NT]), ALU.add))
            after(nc.vector.tensor_tensor(LB[:, :, :], INC[:, :, :].rearrange("p e t -> p t e"),
                                          BANK[7][:, 0:NT * E].rearrange("p (t e) -> p t e", e=E), ALU.add))
            for w in range(TOPK):
                after(nc.vector.tensor_tensor(EQ[:, :, :], OH[:, w], LB[:, :, :], ALU.mult))
                after(nc.vector.tensor_reduce(RED[:, :], EQ[:, :, :], AX.X, ALU.add))
                nc.vector.tensor_copy(POS[:, w], RED[:, :]).then_inc(pos_ready, 1)
                dve.wait_ge(pos_ready, w + 1)
            scales(EARLY)
            hidden(1, 1, 0)
            hidden_low(0, 0)
            copy_xt(3, 1)
            late_largest(EARLY + 1)
            after(nc.vector.tensor_tensor(GE[:, :, :], TILES,
                                          TIL[0:1, 1].rearrange("p (a e) -> p a e", a=1).broadcast_to([1, RT, E]), ALU.is_ge))
            after(nc.vector.tensor_reduce(EIDF[:, :], GE[:, :, 0:E - 1], AX.X, ALU.add))
            nc.vector.tensor_scalar(EID[:, R0:R1], EIDF[:, :], 1.0, None, ALU.add).then_inc(eid_ready, 1)

            for j in range(2, R0):
                if j == 2:
                    hidden_low(1, 1)
                    hidden(2, 0, 0)
                    copy_xt(4, 0)
                    add_y(0, 0)
                else:
                    feed(j, j % 2, 0, add_y, copy_next=j > 3 and j + 1 < R0)
                if j == 7:
                    dve.wait_ge(coef_ready, 1)
                    for w in range(TOPK):
                        after(nc.vector.tensor_tensor(EQ[:, :, :], OH[:, w], SG[:, :, :], ALU.mult))
                        after(nc.vector.tensor_reduce(CW2[:, w], EQ[:, :, :], AX.X, ALU.add))
                for late in VECTOR_LATE.get(j, ()):
                    what, q = late[:-1], int(late[-1])
                    if what == "largest":
                        late_largest(q)
                    elif what == "scale":
                        scales(q)
                    elif what == "low":
                        split_low(q, by_part(late_raw(q)[0]), 3 * EARLY + 2 * (q - EARLY))
                    else:
                        late_down_low(q)

            copy_xt(R0, 0)
            for j in range(R0, R0 + 4):
                e = dve.value_load(EID[0:1, j:j + 1], min_val=0, max_val=NE - 1)
                feed(j, j % 2, e, add_y if j < R0 + 2 else copy_y)
            with in_steps(dve, R0 + 4, R1 - 1, 2) as j:
                for u in range(2):
                    e = dve.value_load(EID[0:1, bass.ds(j + u, 1)], min_val=0, max_val=NE - 1)
                    feed(j + u, u, e, copy_y)
            e = dve.value_load(EID[0:1, R1 - 1:R1], min_val=0, max_val=NE - 1)
            feed(R1 - 1, 0, e, copy_y)

            mark = Count(summed)

            def add_routed(first, end):
                for w in range(TOPK):
                    for i in range(first, end):
                        if w == 0:
                            piece = [n for n, (f, e) in enumerate(PIECES) if f <= i < e][0]
                            dve.wait_ge(routed_loaded[piece], 16 * TOPK)
                            dve.wait_ge(y_copied, i + 1 if i < SH0 else i + RT + 1)
                        done = nc.vector.scalar_tensor_tensor(H[:, i], ROUTED[:, w, i], CW2[:, w, i:i + 1],
                                                              H[:, i], ALU.mult, ALU.add)
                        if w == TOPK - 1:
                            done.then_inc(out_ready, 1)
                        else:
                            mark.up(done)
                    if w == 0:
                        dve.wait_ge(summed, mark.n)

            at = 0
            for j in range(R1, NF):
                feed(j, j % 2, 0, copy_y if j < R1 + 2 else add_y, copy_next=j + 1 < NF)
                if j >= SUM_AT:
                    add_routed(at, at + 3)
                    at += 3
            hidden_low(NF - 1, 1)
            add_y(NF - 2, 0)
            add_y(NF - 1, 1)
            assert at <= POOL_SUMS
            while at < POOL_SUMS:
                add_routed(at, min(at + 2, POOL_SUMS))
                at += 2
            for n, i in enumerate(range(POOL_SUMS, NT)):
                dve.wait_ge(pool_summed, 3 * n + 3)
                dve.wait_ge(y_copied, i + RT + 1)
                nc.vector.tensor_tensor(H[:, i], H[:, i], ROUTED[:, 0, i], ALU.add).then_inc(out_ready, 1)

        @block.gpsimd
        def _(pool):
            nc.gpsimd.memset(ZERO[:, :], 0.0).then_inc(consts_set, 1)

            def inv_sqrt(u, count):
                pool.wait_ge(var_ready, count + 2)
                nc.gpsimd.tensor_tensor(RSTD[:, u], VE[:, u], EPSH[:, 1:2], ALU.pow).then_inc(rstd_ready, 1)

            def all_largest(q):
                wait_apart(pool, am_ready, q + 1, pool_passed)
                nc.gpsimd.partition_all_reduce(AMALL[:, :], AM[:, :], P,
                                               bass.bass_isa.ReduceOp.max).then_inc(amall_ready, 1)

            def split_down_low(q, raw):
                pool.wait_ge(high_ready, 3 * q + 1)
                w = WD[:, bass.ds(q, 1)].rearrange("p a h m n -> p (a h) (m n)")
                nc.gpsimd.tensor_tensor(w[:, 1], raw, w[:, 0].bitcast(F32), ALU.subtract).then_inc(dlow_ready, 1)

            inv_sqrt(0, 0)
            def first_tiles(b):
                q = b // 3
                inv_sqrt(1, b + 1)
                all_largest(q)
                inv_sqrt(2, b + 2)
                split_down_low(q, RAWD[:, bass.ds(q % 2, 1), :].rearrange("p a n -> p (a n)"))
                inv_sqrt(0, b + 3)

            with in_steps(pool, 0, NT - 4, 3) as b:
                first_tiles(b)

            def diff(c):
                if isinstance(c, int):
                    pool.wait_ge(xnt_ready, min(NT, ((c + 1) * CW) // P + 1))
                if not isinstance(c, int) or c >= 2:
                    pool.wait_ge(mixed, 2 * c - 2)
                    pool.wait_ge(kvr_done, 3 * c - 5)
                nc.gpsimd.tensor_tensor(D[:, bass.ds(c % 2, 1)].rearrange("p a k n -> p (a k) n"),
                                        XNT[:, :, bass.ds(c * CW + 1, CW)], XNT[:, :, bass.ds(c * CW, CW)],
                                        ALU.subtract).then_inc(diff_ready, 1)

            def numerator(c):
                pool.wait_ge(exps_ready, 3 * c + 3)
                pool.wait_ge(kvr_copied, 3 * c + 3)
                if not isinstance(c, int) or c >= 1:
                    pool.wait_ge(y_ready, c)
                vs = VS[:, bass.ds(c % 2, 1)].rearrange("p a k n -> p (a k n)")
                nc.gpsimd.tensor_tensor(flat(NUM[:, :, :]), flat(AE[:, 2]), vs, ALU.mult).then_inc(bv_ready, 1)
                pool.wait_ge(pb_ready, c + 1)
                nc.gpsimd.tensor_tensor(flat(T1[:, :, :]), flat(AE[:, 3]), PB[:, 0:KC * CW], ALU.mult)\
                  .then_inc(t1_ready, 1)

            def sum_numerator(c):
                pool.wait_ge(bv_ready, c + 1)
                pool.wait_ge(t1_ready, c + 1)
                nc.gpsimd.tensor_tensor(flat(NUM[:, :, :]), flat(NUM[:, :, :]), flat(T1[:, :, :]), ALU.add)\
                  .then_inc(num_ready, 1)

            def softplus(c):
                rn = RN[:, bass.ds(c % 2, 1)].rearrange("p a k n -> p (a k n)")
                wait_apart(pool, softplus_ready, c + 1, pool_passed)
                nc.gpsimd.tensor_tensor(rn, rn, RE[:, bass.ds(c % 2, 1)].rearrange("p a k n -> p (a k n)"), ALU.add)\
                  .then_inc(rn_ready, 1)

            def sum_exponent(c):
                pool.wait_ge(ln_ready, c + 1)
                wait_apart(pool, rn_ready, c + 1, pool_passed)
                nc.gpsimd.tensor_tensor(flat(DEN[:, :, :]), flat(DEN[:, :, :]),
                                        RN[:, bass.ds(c % 2, 1)].rearrange("p a k n -> p (a k n)"), ALU.add)\
                  .then_inc(s_ready, 1)

            diff(0)
            diff(1)
            first_tiles(NT - 4)
            pool.wait_ge(xnt_ready, NT)

            def chunk(c):
                if not isinstance(c, int) or c + 2 < NC:
                    diff(c + 2)
                softplus(c)
                if isinstance(c, int) and c == NC - 1:
                    inv_sqrt(0, NT)
                    numerator(c)
                    sum_exponent(c)
                    inv_sqrt(1, NT + 1)
                    sum_numerator(c)
                    inv_sqrt(2, NT + 2)
                else:
                    numerator(c)
                    sum_numerator(c)
                    sum_exponent(c)

            chunk(0)
            with pool.Fori(1, NC - 2) as c:
                chunk(c)
            chunk(NC - 2)
            chunk(NC - 1)

            with in_steps(pool, 3, NT - 1, 3) as b:
                for u in range(3):
                    inv_sqrt(u, b + (NT + u))
            inv_sqrt(0, 2 * NT - 1)

            all_largest(EARLY)
            pool.wait_ge(zero_stored, 16)
            pool.wait_ge(rows_set, 1)
            for w in range(TOPK):
                pool.wait_ge(pos_ready, w + 1)
                for i in range(NT):
                    h = int(i >= HALF)
                    if w == 1 and i in (0, HALF):
                        pool.wait_ge(scattered_first[h], 16 * (NT - HALF if h else HALF))
                        tiles = slice(HALF, NT) if h else slice(0, HALF)
                        nc.gpsimd.tensor_copy(XS_ROW[:, tiles], ROWS[:, NT:2 * NT][:, tiles]).then_inc(rows_set, 1)
                        pool.wait_ge(rows_set, 2 + h)
                    if (w, i) in ((0, NT // 4), (1, 0)):
                        all_largest(EARLY + 1 + w)
                    nc.gpsimd.indirect_dma_start(
                        out=xs_slot, out_offset=bass.IndirectOffsetOnAxis(ap=POS[:, w, i:i + 1], axis=0),
                        in_=XS[:, i, :], in_offset=None).then_inc(scattered_second if w else scattered_first[h], 16)

            def keep_rows(k, m):
                wait_apart(pool, xr_loaded[m % 2], 8 * (k - m % 2) + 16, pool_passed)
                if not isinstance(k, int) or k >= 4:
                    wait_apart(pool, y_stored[m % 2], 8 * (k - m % 2) - 16, pool_passed)
                nc.gpsimd.tensor_copy(ROW[:, m:m + 1], XR[:, m % 2, 2 * C:XW].bitcast(I32)).then_inc(row_ready, 1)

            def send_y(k, m):
                wait_apart(pool, row_ready, k + 1, pool_passed)
                if not isinstance(k, int) or k >= 1:
                    wait_apart(pool, y_stored[1 - m % 2], 8 * (k - m % 2) + 16 * (m % 2), pool_passed)
                wait_apart(pool, y_copied, k + (R0 + 1), pool_passed)
                nc.gpsimd.indirect_dma_start(
                    out=y_routed, out_offset=bass.IndirectOffsetOnAxis(ap=ROW[:, m:m + 1], axis=0),
                    in_=Y[:, m % 2], in_offset=None).then_inc(y_stored[m % 2], 16)

            for k in range(4):
                keep_rows(k, k)
                if k >= 2:
                    send_y(k - 2, k - 2)
            with pool.Fori(1, RT // 4) as n:
                for m in range(4):
                    keep_rows(n * 4 + m, m)
                    send_y(n * 4 + (m - 2), (m + 2) % 4)
            keep_rows(RT - 1, (RT - 1) % 4)
            for k in range(RT - 3, RT):
                send_y(k, k % 4)

            for n, i in enumerate(range(POOL_SUMS, NT)):
                piece = [p for p, (f, e) in enumerate(PIECES) if f <= i < e][0]
                pool.wait_ge(routed_loaded[piece], 16 * TOPK)
                nc.gpsimd.tensor_scalar(ROUTED[:, 0, i], ROUTED[:, 0, i], CW2[:, 0, i:i + 1], None, ALU.mult)\
                  .then_inc(pool_summed, 1)
                nc.gpsimd.tensor_scalar(ROUTED[:, 1, i], ROUTED[:, 1, i], CW2[:, 1, i:i + 1], None, ALU.mult)\
                  .then_inc(pool_summed, 1)
                pool.wait_ge(pool_summed, 3 * n + 2)
                nc.gpsimd.tensor_tensor(ROUTED[:, 0, i], ROUTED[:, 0, i], ROUTED[:, 1, i], ALU.add)\
                  .then_inc(pool_summed, 1)


_ORDER = ("x", "w_tok", "w_attn", "chan", "w_gate", "beta", "w_gu", "w_down", "consts")


def build(nc, arrays):
    aps = [nc.dram_tensor(f"in_{n}", arrays[n].shape, mybir.dt.from_np(arrays[n].dtype), kind="ExternalInput").ap()
           for n in _ORDER]
    out = nc.dram_tensor("out_0", (N, C), F32, kind="ExternalOutput").ap()
    vit_block(nc, *aps, out)


def shape_constants():
    c = np.zeros((P, CONSTS), np.float32)
    c[:, 0:P] = np.eye(P)
    c[:, P:2 * P] = np.triu(np.ones((P, P)), 1)
    c[:, 2 * P:3 * P] = 1.0
    c[:, 3 * P:3 * P + E] = E - np.arange(E)
    c[:, 3 * P + E:3 * P + E + NT * E] = np.arange(NT * E) % NT != 0
    c[:, 3 * P + E + NT * E:CONSTS - TOPK * NT] = np.repeat(np.arange(RT), E)
    c[:, CONSTS - TOPK * NT:] = 1 + np.arange(TOPK * NT) * P + np.arange(P)[:, None]
    return c


def lay_out(x, L0_tok_w, L0_tok_b, L0_tok_cls_token, L0_tok_pos, L0_attn_time_decay, L0_attn_time_first,
            L0_attn_time_mix_k, L0_attn_time_mix_v, L0_attn_time_mix_r, L0_attn_W_key, L0_attn_W_value,
            L0_attn_W_receptance, L0_attn_W_output, L0_ffn_gate_w, L0_ffn_beta, L0_ffn_gate_proj_w,
            L0_ffn_up_proj_w, L0_ffn_down_proj_w, L0_ffn_shared_gate_w, L0_ffn_shared_up_w, L0_ffn_shared_down_w):
    f32 = np.float32
    cols = np.zeros((FK * FP, NB, S), f32)
    patches = np.asarray(x).reshape(NB, 3, GRID, PATCH, GRID, PATCH).transpose(1, 3, 5, 0, 2, 4)
    cols[0:F, :, 2:] = patches.reshape(F, NB, NPATCH)
    for t in range(T):
        cols[F + t, :, t + 1] = 1.0
    cols[F + T, :, 2:] = 1.0
    cols[F + T + 1, :, 1] = 1.0
    rows = np.zeros((FK * FP, C), f32)
    rows[0:F] = np.asarray(L0_tok_w).T
    rows[F:F + T] = L0_tok_pos
    rows[F + T] = L0_tok_b
    rows[F + T + 1] = L0_tok_cls_token

    def by_partition(a, *tail):
        a = np.asarray(a)
        return a.reshape(-1, P, *a.shape[1:]).swapaxes(0, 1)

    chan = [np.asarray(v).reshape(C) for v in (L0_attn_time_decay, L0_attn_time_first, L0_attn_time_mix_k,
                                               L0_attn_time_mix_v, L0_attn_time_mix_r)]
    attn = [np.asarray(w).T for w in (L0_attn_W_key, L0_attn_W_value, L0_attn_W_receptance, L0_attn_W_output)]
    gates = np.concatenate([L0_ffn_shared_gate_w, L0_ffn_gate_proj_w])
    ups = np.concatenate([L0_ffn_shared_up_w, L0_ffn_up_proj_w])
    downs = np.concatenate([L0_ffn_shared_down_w, L0_ffn_down_proj_w])
    gu = np.stack([gates, ups], 1).reshape(NE, 2, KC, P, M).transpose(0, 3, 1, 2, 4)
    arrays = {
        "x": cols.reshape(FK, FP, NT, P).transpose(2, 1, 0, 3),
        "w_tok": rows.reshape(FK, FP, C).transpose(1, 0, 2),
        "w_attn": np.stack([by_partition(w) for w in attn], 1),
        "chan": np.stack([by_partition(v) for v in chan], 1),
        "w_gate": by_partition(np.asarray(L0_ffn_gate_w).T),
        "beta": np.broadcast_to(np.asarray(L0_ffn_beta), (P, E)),
        "w_gu": gu.reshape(NE, P, 2 * KC * M),
        "w_down": downs.reshape(NE, MC, P, C).transpose(0, 2, 1, 3).reshape(NE, P, MC * C),
        "consts": shape_constants(),
    }
    return {k: np.ascontiguousarray(v) for k, v in arrays.items()}


def kernel(**inputs):
    import concourse.bacc as bacc
    from concourse.bass_utils import run_bass_kernel_spmd as run

    arrays = lay_out(**inputs)
    nc = bacc.Bacc("TRN2", target_bir_lowering=False, num_devices=1)
    build(nc, arrays)
    r = run(nc, [{f"in_{n}": a for n, a in arrays.items()}], core_ids=[0])
    return r.results[0]["out_0"].reshape(NB, S, C)[:, 1:]
```
